# Optimizing a Trainium2 kernel written in Bass

```python
import numpy as np
import jax
import jax.numpy as jnp

def _softmax(x, axis=-1):
    return jax.nn.softmax(x, axis=axis)

def _gelu(x):
    return jax.nn.gelu(x, approximate=True)

def _silu(x):
    return jax.nn.silu(x)

def _sigmoid(x):
    return jax.nn.sigmoid(x)

def _layernorm(x, axis=-1, eps=1e-05):
    m = jnp.mean(x, axis=axis, keepdims=True)
    v = jnp.var(x, axis=axis, keepdims=True)
    return (x - m) / jnp.sqrt(v + eps)

def _scatter_add(tgt, idx, src, axis=0):
    return tgt.at[idx].add(src)

def _segment_sum(src, seg, n):
    return jax.ops.segment_sum(src, seg, n)
kernel_name = 'mk_gnn_preln_d2_gnn_r8_89a80f'

def setup_inputs(seed: int=0):
    np.random.seed(seed)
    _w = jnp.asarray

    def _rec_inputs():
        import jax
        import jax.numpy as jnp
        _gk = jax.random.key(seed)
        x = -0.0005121 + 1.001 * jax.random.normal(jax.random.fold_in(_gk, 1), (6250, 64), jnp.float32)
        _s = jax.random.randint(jax.random.fold_in(_gk, 2), (100000,), 0, 6250, jnp.int32)
        _d = jax.random.randint(jax.random.fold_in(_gk, 3), (100000,), 0, 6250, jnp.int32)
        _loop = jnp.arange(6250, dtype=jnp.int32)
        src = jnp.concatenate([_s, _d, _loop])
        dst = jnp.concatenate([_d, _s, _loop])
        _o = jnp.argsort(dst, stable=True)
        src = src[_o]
        dst = dst[_o]
        edge_attr_64 = 0.000189758 + 1.00013 * jax.random.normal(jax.random.fold_in(_gk, 11), (206250, 64), jnp.float32)
        edge_weight = jax.random.uniform(jax.random.fold_in(_gk, 13), (206250,), jnp.float32, 0.0, 0.999998)
        return (x, src, dst, edge_attr_64, edge_weight)
    x, src, dst, edge_attr_64, edge_weight = _rec_inputs()

    def _L0_gnn_setup():
        import jax, jax.numpy as jnp
        import numpy as np
        N, E = (6250, 100000)
        NODE_D, EDGE_D, HID = (64, 64, 64)
        key = jax.random.key(seed)
        ks = jax.random.split(key, 12)
        node_features = jax.random.normal(ks[0], (N, NODE_D), dtype=jnp.float32)
        edge_index = jax.random.randint(ks[1], (2, E), 0, N, dtype=jnp.int64)
        edge_features = jax.random.normal(ks[2], (E, EDGE_D), dtype=jnp.float32)
        s = 0.05
        W1 = jax.random.normal(ks[3], (NODE_D + EDGE_D, HID), dtype=jnp.float32) * s
        b1 = jax.random.normal(ks[4], (HID,), dtype=jnp.float32) * s
        W2 = jax.random.normal(ks[5], (HID, HID), dtype=jnp.float32) * s
        b2 = jax.random.normal(ks[6], (HID,), dtype=jnp.float32) * s
        U1 = jax.random.normal(ks[7], (NODE_D + HID, HID), dtype=jnp.float32) * s
        c1 = jax.random.normal(ks[8], (HID,), dtype=jnp.float32) * s
        U2 = jax.random.normal(ks[9], (HID, NODE_D), dtype=jnp.float32) * s
        c2 = jax.random.normal(ks[10], (NODE_D,), dtype=jnp.float32) * s
        return {'node_features': node_features, 'edge_index': edge_index, 'edge_features': edge_features, 'W1': W1, 'b1': b1, 'W2': W2, 'b2': b2, 'U1': U1, 'c1': c1, 'U2': U2, 'c2': c2}
    _L0_gnn_all = _L0_gnn_setup()
    _L0_gnn_in = {k: v for k, v in _L0_gnn_all.items() if k in ('W1', 'b1', 'W2', 'b2', 'U1', 'c1', 'U2', 'c2')}
    del _L0_gnn_all

    def _L1_gnn_setup():
        import jax, jax.numpy as jnp
        import numpy as np
        N_NODES = 6250
        N_EDGES = 100000
        D_FEAT = 64
        key = jax.random.key(seed)
        k1, k2, k3 = jax.random.split(key, 3)
        x = jax.random.normal(k1, (N_NODES, D_FEAT), dtype=jnp.float32)
        eidx = jax.random.randint(k2, (2, N_EDGES), 0, N_NODES, dtype=jnp.int64)
        enorm = jax.random.uniform(k3, (N_EDGES,), dtype=jnp.float32)
        return {'x': x, 'eidx': eidx, 'enorm': enorm}
    _L1_gnn_all = _L1_gnn_setup()
    _L1_gnn_in = {k: v for k, v in _L1_gnn_all.items() if k in ()}
    del _L1_gnn_all
    return {'x': x, 'src': src, 'dst': dst, 'edge_attr_64': edge_attr_64, 'edge_weight': edge_weight, 'L0_gnn_W1': _L0_gnn_in['W1'], 'L0_gnn_b1': _L0_gnn_in['b1'], 'L0_gnn_W2': _L0_gnn_in['W2'], 'L0_gnn_b2': _L0_gnn_in['b2'], 'L0_gnn_U1': _L0_gnn_in['U1'], 'L0_gnn_c1': _L0_gnn_in['c1'], 'L0_gnn_U2': _L0_gnn_in['U2'], 'L0_gnn_c2': _L0_gnn_in['c2']}

def reference(x, src, dst, edge_attr_64, edge_weight, L0_gnn_W1, L0_gnn_b1, L0_gnn_W2, L0_gnn_b2, L0_gnn_U1, L0_gnn_c1, L0_gnn_U2, L0_gnn_c2):
    import jax
    import jax.numpy as jnp

    def _L0_gnn_ref(node_features, edge_index, edge_features, W1, b1, W2, b2, U1, c1, U2, c2):
        import jax, jax.numpy as jnp
        import numpy as np
        N, E = (6250, 100000)
        NODE_D, EDGE_D, HID = (64, 64, 64)
        src = edge_index[0]
        dst = edge_index[1]
        src_features = node_features[src]
        msg_input = jnp.concatenate([src_features, edge_features], axis=-1)
        h = jax.nn.relu(msg_input @ W1 + b1)
        messages = h @ W2 + b2
        aggregated = jax.ops.segment_sum(messages, dst, num_segments=node_features.shape[0])
        update_input = jnp.concatenate([node_features, aggregated], axis=-1)
        g = jax.nn.relu(update_input @ U1 + c1)
        new_node_features = g @ U2 + c2
        return new_node_features

    def _L1_gnn_ref(x, eidx, enorm):
        import jax, jax.numpy as jnp
        import numpy as np
        N_NODES = 6250
        N_EDGES = 100000
        D_FEAT = 64
        sidx, tidx = (eidx[0], eidx[1])
        message = x[sidx] * enorm[:, None]
        res = jax.ops.segment_sum(message, tidx, num_segments=x.shape[0])
        return res
    edge_index = jnp.stack([src, dst])
    h = jnp.maximum(_layernorm(x, axis=-1), 0.0)
    x = x + _L0_gnn_ref(h, edge_index, edge_attr_64, L0_gnn_W1, L0_gnn_b1, L0_gnn_W2, L0_gnn_b2, L0_gnn_U1, L0_gnn_c1, L0_gnn_U2, L0_gnn_c2)
    h = jnp.maximum(_layernorm(x, axis=-1), 0.0)
    x = x + _L1_gnn_ref(h, edge_index, edge_weight)
    return x

_drawn_inputs = setup_inputs


def setup_inputs(seed=0):
    import zlib

    import numpy as np

    out = dict(_drawn_inputs(seed))
    spreads = {}
    factors = {'edge_attr_64': 3.034, 'L0_gnn_c1': 4.032, 'L0_gnn_b1': 2.75}
    for name, (base, spread) in spreads.items():
        noise = np.random.default_rng([zlib.crc32(name.encode()), seed]).standard_normal(out[name].shape)
        drawn = base * np.exp(spread * noise) if base else spread * noise
        out[name] = jnp.asarray(drawn.astype(out[name].dtype))
    for name, factor in factors.items():
        out[name] = (out[name] * factor).astype(out[name].dtype)
    return out
```

```python
from contextlib import ExitStack

import concourse.bass as bass
from concourse import mybir

ALU = mybir.AluOpType
ACT = mybir.ActivationFunctionType
F32 = mybir.dt.float32
I32 = mybir.dt.int32
AX_X = mybir.AxisListType.X
ds = bass.ds

P = 128
D = 64
T = 8
GE = P * T
W = 48
RING = 3
NP = 125
BLK = 5
CN = NP * BLK
BC = BLK * D
FAR = -20000.0


def steps(eng, count, unroll, body):
    assert count % unroll == 0
    for slot in range(unroll):
        body(slot, slot)
    with eng.Fori(1, count // unroll) as turn:
        for slot in range(unroll):
            body(turn * unroll + slot, slot)


def wait_step(eng, sem, g, each=1):
    if not isinstance(g, int) or g >= 0:
        eng.wait_ge(sem, (g + 1) * each)


def build(nc, x, src, dst, edge_attr, edge_weight, w1, b1, w2, b2, u1, c1, u2, c2, out):
    N = x.shape[0]
    E = src.shape[0]
    NB = N // NP
    CHUNKS = NB // BLK
    FULL = E // GE
    GROUPS = FULL + 1
    OVERLAP = FULL * GE - (E - GE)
    HALF_A = GROUPS - 97
    HALF = (HALF_A, GROUPS - HALF_A)
    PARAMETERS = 11
    WINDOWS = -(-N // W)
    assert N == NB * NP and NB == CHUNKS * BLK and CHUNKS % 2 == 0 and FULL % RING == 0

    table1 = nc.dram_tensor("table1", (N, D), F32, kind="Internal").ap()
    table2 = nc.dram_tensor("table2", (N, D), F32, kind="Internal").ap()

    with ExitStack() as ctx:
        def sb(name, shape, dt=F32):
            return ctx.enter_context(nc.sbuf_tensor(name, shape, dt))

        def psum(name, shape):
            return ctx.enter_context(nc.psum_tensor(name, shape, F32))

        def sem(name):
            return ctx.enter_context(nc.semaphore(name))

        x_all = sb("x_all", [NP, NB * D])
        cent = sb("cent", [NP, NB * D])
        row_sum = sb("row_sum", [NP, NB])
        mean = sb("mean", [NP, NB])
        var = sb("var", [NP, NB])
        std = sb("std", [NP, NB])
        rstd = sb("rstd", [NP, NB])
        h_stage = sb("h_stage", [NP, 2, BC])
        row_stage = sb("row_stage", [NP, 2, BC])
        node_cols = sb("node_cols", [P, N])
        hT = node_cols[0:D + 1, :]
        sq = node_cols[0:NP, 0:NB * D]
        acc1 = sb("acc1", [D + 1, N + W])
        late = sb("late", [P, N + W])
        acc2 = late[0:D, :]
        t_stage = sb("t_stage", [D, 2, CN])
        early = late[:, 0:6 * GE].rearrange("g (k h e) -> g k h e", k=3, h=2)
        wgt_g = early[:, 0]
        dst_i = early[:, 1].bitcast(I32)
        src_i = early[:, 2].bitcast(I32)
        key_g = sb("key_g", [P, GE])
        hi = sb("hi", [P, 2])
        lo = sb("lo", [P, 2])
        base = sb("base", [P, 2])
        bad = sb("bad", [P, 2])
        above = sb("above", [P, 2])
        bad_all = sb("bad_all", [P, 1])
        fast_f = sb("fast_f", [P, 1])
        fast_i = sb("fast_i", [P, 1], I32)
        base_row = sb("base_row", [1, GROUPS], I32)
        rel = sb("rel", [P, GROUPS, T])
        idx = sb("idx", [P, GROUPS + RING, T], I32)
        wgt = sb("wgt", [P, GROUPS, T])
        idx_ring = sb("idx_ring", [P, RING, T], I32)
        ea_ring = sb("ea_ring", [P, RING, T * D])
        eaT = sb("eaT", [P, RING, T // 2, P])
        rows = sb("rows", [P, RING, T, D])
        pre = sb("pre", [P, RING, T, D])
        hid = sb("hid", [P, RING, T, D + 1])
        hot = sb("hot", [P, RING, T, W])
        key_now = sb("key_now", [P, RING, T])
        ident = sb("ident", [P, P])
        ones = sb("ones", [P, P])
        iota = sb("iota", [P, W])
        eps = sb("eps", [P, 1])
        w1a = sb("w1a", [D, D])
        w1b2 = sb("w1b2", [P, P])
        w2b = sb("w2b", [D + 1, D])
        w2bT = sb("w2bT", [D, D + 1])
        w2u = sb("w2u", [D + 1, D])
        u1a = sb("u1a", [D + 1, D])
        u1b = sb("u1b", [D, D])
        u2_s = sb("u2_s", [D, D])
        b1_bc = sb("b1_bc", [NP, D])
        c2_bc = sb("c2_bc", [NP, D])

        pair = [psum(f"pair{i}", [P, 2, 512]) for i in range(4)]

        def wide(slot):
            return pair[slot][0:D, :, :].rearrange("f b n -> f (b n)")[:, 0:BLK * P].rearrange(
                "f (b n) -> f b n", n=P)

        def tall(slot):
            return pair[2][0:NP, slot, 0:BC]

        x_loaded = sem("x_loaded")
        src_loaded = sem("src_loaded")
        dst_loaded = sem("dst_loaded")
        wgt_loaded = sem("wgt_loaded")
        par_loaded = sem("par_loaded")
        consts_set = sem("consts_set")
        pool_step = sem("pool_step")
        pe_held = sem("pe_held")
        pool_held = sem("pool_held")
        ones_set = sem("ones_set")
        key_made = sem("key_made")
        key_turned = sem("key_turned")
        key_kept = sem("key_kept")
        range_made = sem("range_made")
        bad_made = sem("bad_made")
        bad_summed = sem("bad_summed")
        fast_made = sem("fast_made")
        base_turned = sem("base_turned")
        base_made = sem("base_made")
        w2_turned = sem("w2_turned")
        w2_kept = sem("w2_kept")
        w2u_made = sem("w2u_made")
        w2u_kept = sem("w2u_kept")
        ln_sum = sem("ln_sum")
        ln_mean = sem("ln_mean")
        ln_cent = sem("ln_cent")
        ln_sq = sem("ln_sq")
        ln_var = sem("ln_var")
        ln_std = sem("ln_std")
        ln_rstd = sem("ln_rstd")
        ln_norm = sem("ln_norm")
        h_staged = sem("h_staged")
        h_turned = sem("h_turned")
        hT_staged = sem("hT_staged")
        hT_kept = sem("hT_kept")
        t1_made = sem("t1_made")
        t1_staged = sem("t1_staged")
        t1_stored = [sem(f"t1_stored{s}") for s in range(2)]
        acc2_set = sem("acc2_set")
        c2_added = sem("c2_added")
        idx_ready = sem("idx_ready")
        gathered = [sem(f"gathered{s}") for s in range(RING)]
        ea_loaded = [sem(f"ea_loaded{s}") for s in range(RING)]
        ea_turned = sem("ea_turned")
        eaT_kept = sem("eaT_kept")
        q_made = sem("q_made")
        pre_made = sem("pre_made")
        hid_made = sem("hid_made")
        hot_made = sem("hot_made")
        hot_weighed = sem("hot_weighed")
        seg_made = sem("seg_made")
        acc_added = sem("acc_added")
        turn_made = sem("turn_made")
        group_done = sem("group_done")
        above_made = sem("above_made")
        bad_counted = sem("bad_counted")
        last_made = sem("last_made")
        key_moved = sem("key_moved")
        whot_made = sem("whot_made")
        whot_weighed = sem("whot_weighed")
        wseg_made = sem("wseg_made")
        wacc_added = sem("wacc_added")
        g_made = sem("g_made")
        g_staged = sem("g_staged")
        up_made = sem("up_made")
        x1_made = sem("x1_made")
        h2_staged = sem("h2_staged")
        t2_stored = [sem(f"t2_stored{s}") for s in range(2)]
        a_staged = sem("a_staged")
        a_turned = sem("a_turned")
        out_staged = sem("out_staged")
        out_stored = [sem(f"out_stored{s}") for s in range(2)]

        def blocks(dram, c):
            return dram[ds(c * CN, CN), :].rearrange("(b p) f -> p b f", p=NP)

        def chunked(t, c):
            return t[:, ds(c * BC, BC)]

        def by_block(ap):
            return ap.rearrange("p (b f) -> p b f", f=D)

        def spread(ap, n):
            return ap.rearrange("p (b o) -> p b o", o=1).to_broadcast([ap.shape[0], ap.shape[1], n])

        def group_rows(dram, h):
            g0, n = (0, HALF[0]) if h == 0 else (HALF[0], HALF[1] - 1)
            return dram[g0 * GE:(g0 + n) * GE].rearrange("(g e) -> g e", e=GE), n

        def edge_row(g):
            return E - GE if isinstance(g, int) and g == FULL else g * GE

        def gathered_wait(eng, g, slot, before):
            turns = -(-(before - slot) // RING) if before else 0
            if isinstance(g, int):
                eng.wait_ge(gathered[slot], (g // RING + 1 + turns) * 16 * T)
            else:
                eng.wait_ge(gathered[slot], ((g - slot) // RING + 1 + turns) * 16 * T)

        block = ctx.enter_context(nc.Block())

        @block.sync
        def _(sp):
            sp.dma_start(by_block(x_all[:, :]), x.rearrange("(b p) f -> p b f", p=NP)).then_inc(x_loaded, 16)

            def load_groups(tile, dram, loaded):
                for h in range(2):
                    source, n = group_rows(dram, h)
                    sp.dma_start(tile[0:n, h, :], source).then_inc(loaded, 16)
                n = HALF[1] - 1
                sp.dma_start(tile[n:n + 1, 1, :],
                             dram[E - GE:E].rearrange("(o e) -> o e", o=1)).then_inc(loaded, 16)

            load_groups(src_i, src, src_loaded)
            load_groups(dst_i, dst, dst_loaded)
            load_groups(wgt_g, edge_weight, wgt_loaded)

            def load_ea(g, slot):
                wait_step(sp, ea_turned, g - RING)
                rows_of = edge_attr[ds(edge_row(g), GE), :].rearrange("(p t) f -> p (t f)", t=T)
                sp.dma_start(ea_ring[:, slot, :], rows_of).then_inc(ea_loaded[slot], 16)

            def store_t1(c, slot):
                wait_step(sp, t1_staged, c)
                sp.dma_start(blocks(table1, c), by_block(row_stage[:, slot, :])).then_inc(t1_stored[slot], 16)

            steps(sp, CHUNKS, 2, store_t1)
            steps(sp, FULL, RING, load_ea)
            load_ea(FULL, 0)

            def store_t2(c, slot):
                wait_step(sp, h2_staged, c)
                sp.dma_start(blocks(table2, c), by_block(h_stage[:, slot, :])).then_inc(t2_stored[slot], 16)

            steps(sp, CHUNKS, 2, store_t2)

            def store_out(c, slot):
                wait_step(sp, out_staged, c)
                sp.dma_start(blocks(out, c), by_block(row_stage[:, slot, :])).then_inc(out_stored[slot], 16)

            steps(sp, CHUNKS, 2, store_out)
            for s in range(2):
                sp.wait_ge(t1_stored[s], 16 * CHUNKS // 2)
                sp.wait_ge(t2_stored[s], 16 * CHUNKS // 2)
                sp.wait_ge(out_stored[s], 16 * CHUNKS // 2)

        @block.gpsimd
        def _(pool):
            pool.memset(eps[:, :], 1e-5).then_inc(consts_set, 1)
            pool.memset(ones[:, :], 1.0).then_inc(consts_set, 1)
            pool.memset(ident[:, :], 0.0).then_inc(pool_step, 1)
            pool.memset(w1b2[:, :], 0.0).then_inc(pool_step, 1)
            pool.wait_ge(pool_step, 2)
            pool.affine_select(out=ident[:, :], in_=ident[:, :], compare_op=ALU.not_equal, fill=1.0, base=0,
                               pattern=[[-1, P]], channel_multiplier=1).then_inc(consts_set, 1)
            pool.iota(iota[:, :], [[1, W]], base=0, channel_multiplier=0,
                      allow_small_or_imprecise_dtypes=True).then_inc(consts_set, 1)
            pool.memset(bad[:, :], 0.0).then_inc(consts_set, 1)
            for to, of in ((w1a[:, :], w1[0:D, :]), (w1b2[0:D, 0:D], w1[D:2 * D, :]),
                           (w1b2[D:P, D:P], w1[D:2 * D, :]), (w2b[0:D, :], w2),
                           (w2b[D:D + 1, :], b2.rearrange("(o f) -> o f", o=1)),
                           (u1a[0:D, :], u1[0:D, :]), (u1b[:, :], u1[D:2 * D, :]), (u2_s[:, :], u2),
                           (u1a[D:D + 1, :], c1.rearrange("(o f) -> o f", o=1)),
                           (b1_bc[:, :], b1.rearrange("(o f) -> o f", o=1).to_broadcast([NP, D])),
                           (c2_bc[:, :], c2.rearrange("(o f) -> o f", o=1).to_broadcast([NP, D]))):
                pool.dma_start(to, of).then_inc(par_loaded, 16)
            pool.memset(hid[:, :, :, D:D + 1], 1.0).then_inc(consts_set, 1)
            pool.memset(idx[:, GROUPS:, :], 0).then_inc(consts_set, 1)
            pool.memset(acc1[:, :], 0.0).then_inc(consts_set, 1)

            def gather(table, g, slot, used, before, refills):
                wait_step(pool, idx_ready, g + refills)
                wait_step(pool, used, g - RING + before)
                pool.sem_inc(pool_held, 1)
                for t in range(T):
                    pool.indirect_dma_start(
                        out=rows[:, slot, t, :], out_offset=None, in_=table,
                        in_offset=bass.IndirectOffsetOnAxis(ap=idx_ring[:, slot, t:t + 1], axis=0),
                    ).then_inc(gathered[slot], 16)

            pool.wait_ge(ln_var, 1)
            pool.memset(hT[D:D + 1, :], 1.0).then_inc(ones_set, 1)
            for s in range(2):
                pool.wait_ge(t1_stored[s], 16 * CHUNKS // 2)
            steps(pool, FULL, RING, lambda g, slot: gather(table1, g, slot, pre_made, 0, 0))
            gather(table1, FULL, 0, pre_made, 0, 0)
            pool.wait_ge(pre_made, GROUPS)
            for s in range(2):
                pool.wait_ge(t2_stored[s], 16 * CHUNKS // 2)
            steps(pool, FULL, RING, lambda g, slot: gather(table2, g, slot, group_done, GROUPS, GROUPS + RING))
            gather(table2, FULL, 0, group_done, GROUPS, GROUPS + RING)

        @block.scalar
        def _(act):
            def layer_norm(n):
                act.wait_ge(ln_cent, n)
                act.activation(sq[:, :], cent[:, :], ACT.Square).then_inc(ln_sq, 1)
                act.wait_ge(ln_var, n)
                act.activation(std[:, :], var[:, :], ACT.Sqrt, bias=eps[0:NP, :], scale=1.0 / D).then_inc(ln_std, 1)
                act.wait_ge(ln_norm, n)

            def refill_idx(g, slot):
                act.copy(idx_ring[:, slot, :], idx[:, ds(g, 1), :].rearrange("p o t -> p (o t)")
                         if not isinstance(g, int) else idx[:, g, :]).then_inc(idx_ready, 1)

            act.wait_ge(consts_set, 1)
            layer_norm(1)

            def stage_h(c, slot):
                wait_step(act, h_turned, c - 2)
                act.activation(h_stage[:, slot, :], chunked(cent, c), ACT.Relu).then_inc(h_staged, 1)
                wait_step(act, h_turned, c)
                wait_step(act, t1_made, c - 2)
                wait_step(act, hT_kept, c - 2)
                act.copy(t_stage[:, slot, :].rearrange("f (b n) -> f b n", n=NP),
                         wide(slot)[:, :, 0:NP]).then_inc(hT_staged, 1)

            steps(act, CHUNKS, 2, stage_h)

            act.wait_ge(consts_set, 8)
            act.wait_ge(key_kept, 4)
            for s in range(RING):
                refill_idx(s, s)

            def pass1(g, slot):
                wait_step(act, ea_turned, g)
                wait_step(act, q_made, g - RING)
                act.copy(eaT[:, slot, :, :].rearrange("p a e -> p (a e)"), pair[slot][:, 0, :]).then_inc(eaT_kept, 1)
                wait_step(act, pre_made, g)
                wait_step(act, group_done, g - RING)
                act.activation(hid[:, slot, :, 0:D], pre[:, slot, :, :], ACT.Relu).then_inc(hid_made, 1)
                refill_idx(g + RING, slot)

            steps(act, FULL, RING, pass1)
            pass1(FULL, 0)

            def stage_g(c, slot):
                wait_step(act, g_made, c)
                wait_step(act, up_made, c - 2)
                act.activation(t_stage[:, slot, :].rearrange("f (b n) -> f b n", n=NP), wide(slot)[:, :, 0:NP],
                               ACT.Relu).then_inc(g_staged, 1)

            steps(act, CHUNKS, 2, stage_g)
            layer_norm(2)

            def stage_h2(c, slot):
                if not isinstance(c, int):
                    act.wait_ge(t2_stored[slot], (c - slot) * 8)
                act.activation(h_stage[:, slot, :], chunked(cent, c), ACT.Relu).then_inc(h2_staged, 1)

            steps(act, CHUNKS, 2, stage_h2)

            for s in range(RING):
                refill_idx(s, s)

            def pass2(g, slot):
                wait_step(act, group_done, g + GROUPS)
                refill_idx(g + RING, slot)

            steps(act, FULL, RING, pass2)
            act.wait_ge(turn_made, 2)

            def stage_a(c, slot):
                wait_step(act, a_turned, c - 2)
                act.copy(t_stage[:, slot, :], acc2[:, ds(c * CN, CN)]).then_inc(a_staged, 1)

            steps(act, CHUNKS, 2, stage_a)

        @block.tensor
        def _(pe):
            def hold():
                pe.sem_inc(pe_held, 1)

            pe.wait_ge(consts_set, 5)
            pe.wait_ge(par_loaded, 16 * PARAMETERS)

            pe.transpose(pair[3][0:D, 0, 0:D + 1], w2b[:, :], ident[0:D + 1, 0:D + 1]).then_inc(w2_turned, 1)
            pe.wait_ge(w2_kept, 1)
            pe.matmul(pair[3][0:D + 1, 1, 0:D], w2bT[:, :], u1b[:, :], start=True, stop=True).then_inc(w2u_made, 1)
            pe.wait_ge(w2u_kept, 1)

            def turn(k):
                h = k % 2
                n = HALF[h]
                if k < 4:
                    pe.wait_ge(key_made, k + 1)
                for q in range(2):
                    if 2 * k + q >= 2:
                        pe.wait_ge(key_kept, 2 * k + q - 1)
                    for t in range(4):
                        source = (key_g if k < 4 else wgt_g[:, h, :])[0:n, :].rearrange("g (p t) -> g t p", t=T)[:, 4 * q + t, :]
                        last = pe.transpose(pair[3][:, q, t * P:t * P + n], source, ident[0:n, 0:n])
                    last.then_inc(key_turned, 1)

            for k in range(2):
                turn(k)

            def chunk1(c, slot):
                wait_step(pe, h_staged, c)
                wait_step(pe, hT_staged, c - 2)
                hold()
                for b in range(BLK):
                    last = pe.transpose(wide(slot)[:, b, 0:NP], h_stage[:, slot, b * D:(b + 1) * D],
                                        ident[0:NP, 0:NP])
                last.then_inc(h_turned, 1)
                wait_step(pe, hT_staged, c)
                wait_step(pe, t1_staged, c - 2)
                for b in range(BLK):
                    last = pe.matmul(tall(slot)[:, b * D:(b + 1) * D], t_stage[:, slot, b * NP:(b + 1) * NP],
                                     w1a[:, :], start=True, stop=True)
                last.then_inc(t1_made, 1)

            steps(pe, CHUNKS, 2, chunk1)

            pe.wait_ge(key_kept, 4)
            pe.wait_ge(bad_made, 2)
            pe.matmul(pair[3][:, 0, 0:2], ones[:, :], bad[:, :], start=True, stop=True).then_inc(bad_summed, 1)
            for h in range(2):
                pe.wait_ge(range_made, 3 * 2 + 1 + h)
                pe.transpose(pair[3][0:1, 1, h * P:h * P + HALF[h]], base[0:HALF[h], h:h + 1],
                             ident[0:HALF[h], 0:HALF[h]]).then_inc(base_turned, 1)
            pe.wait_ge(base_made, 1)
            for k in range(2, 4):
                turn(k)
            pe.wait_ge(wgt_loaded, 48)
            for k in range(4, 6):
                turn(k)
            pe.wait_ge(key_kept, 12)
            pe.wait_ge(consts_set, 8)

            pe.wait_ge(fast_made, 2)
            fast = pe.value_load(fast_i[0:1, 0:1], min_val=0, max_val=1)

            def products(g, slot):
                pe.wait_ge(ea_loaded[slot], g // RING * 16 + 16) if isinstance(g, int) else \
                    pe.wait_ge(ea_loaded[slot], (g - slot) // RING * 16 + 16)
                wait_step(pe, eaT_kept, g - RING)
                for a in range(T // 2):
                    last = pe.transpose(pair[slot][:, 0, a * P:(a + 1) * P],
                                        ea_ring[:, slot, a * P:(a + 1) * P], ident[:, :])
                last.then_inc(ea_turned, 1)
                wait_step(pe, eaT_kept, g)
                wait_step(pe, pre_made, g - RING)
                for a in range(T // 2):
                    last = pe.matmul(pair[slot][:, 1, a * P:(a + 1) * P], eaT[:, slot, a, :], w1b2[:, :],
                                     start=True, stop=True)
                last.then_inc(q_made, 1)

            def segment(lhs, slot, bank, m):
                for t in range(T):
                    last = pe.matmul(pair[3][0:m, bank, 0:W], lhs[:, slot, t, 0:m], hot[:, slot, t, :],
                                     start=(t == 0), stop=(t == T - 1))
                return last

            def fast1(g, slot):
                products(g, slot)
                wait_step(pe, hot_made, g)
                wait_step(pe, hid_made, g)
                wait_step(pe, acc_added, g - 1)
                segment(hid, slot, 0, D + 1).then_inc(group_done, 1)

            def fast2(g, slot):
                wait_step(pe, hot_weighed, g)
                gathered_wait(pe, g, slot, GROUPS)
                wait_step(pe, acc_added, g + GROUPS - 1)
                segment(rows, slot, 0, D).then_inc(group_done, 1)

            def slow1(g, slot):
                products(g, slot)
                wait_step(pe, hid_made, g)
                windows(lambda: segment(hid, slot, 0, D + 1), whot_made, g, g)

            def slow2(g, slot):
                gathered_wait(pe, g, slot, GROUPS)
                windows(lambda: segment(rows, slot, 0, D), whot_weighed, g, g + GROUPS)

            def windows(product, made, g_made, g_done):
                hold()
                with pe.Fori(0, WINDOWS) as k:
                    pe.wait_ge(made, g_made * WINDOWS + k + 1)
                    product().then_inc(wseg_made, 1)
                    pe.wait_ge(wacc_added, g_done * WINDOWS + k + 1)
                pe.nop().then_inc(group_done, 1)

            with pe.If(fast > 0):
                steps(pe, FULL, RING, fast1)
                fast1(FULL, 0)
            with pe.Else():
                steps(pe, FULL, RING, slow1)
                slow1(FULL, 0)

            pe.wait_ge(turn_made, 1)
            pe.wait_ge(ones_set, 1)
            def chunk2(c, slot):
                wait_step(pe, g_staged, c - 2)
                for b0, nb in ((0, 4), (4, 1)):
                    to = wide(slot)[:, b0:b0 + nb, 0:NP]
                    pe.matmul(to, u1a[:, :], hT[:, ds(c * CN + b0 * NP, nb * NP)].rearrange("f (b n) -> f b n", n=NP),
                              start=True, stop=False)
                    last = pe.matmul(to, w2u[:, :],
                                     acc1[:, ds(c * CN + b0 * NP, nb * NP)].rearrange("f (b n) -> f b n", n=NP),
                                     start=False, stop=True)
                last.then_inc(g_made, 1)
                wait_step(pe, g_staged, c)
                wait_step(pe, x1_made, c - 2)
                for b in range(BLK):
                    last = pe.matmul(tall(slot)[:, b * D:(b + 1) * D], t_stage[:, slot, b * NP:(b + 1) * NP],
                                     u2_s[:, :], start=True, stop=True)
                last.then_inc(up_made, 1)

            steps(pe, CHUNKS, 2, chunk2)

            with pe.If(fast > 0):
                steps(pe, FULL, RING, fast2)
                fast2(FULL, 0)
            with pe.Else():
                steps(pe, FULL, RING, slow2)
                slow2(FULL, 0)

            def chunk3(c, slot):
                wait_step(pe, a_staged, c)
                wait_step(pe, out_staged, c - 2)
                hold()
                for b in range(BLK):
                    last = pe.transpose(tall(slot)[:, b * D:(b + 1) * D], t_stage[:, slot, b * NP:(b + 1) * NP],
                                        ident[0:D, 0:D])
                last.then_inc(a_turned, 1)

            steps(pe, CHUNKS, 2, chunk3)

        @block.vector
        def _(dve):
            def layer_norm(n):
                xv, cv = by_block(x_all[:, :]), by_block(cent[:, :])
                dve.tensor_reduce(row_sum[:, :], xv, AX_X, ALU.add).then_inc(ln_sum, 1)
                dve.wait_ge(ln_sum, n)
                dve.tensor_scalar(mean[:, :], row_sum[:, :], 1.0 / D, None, ALU.mult).then_inc(ln_mean, 1)
                dve.wait_ge(ln_mean, n)
                dve.tensor_tensor(cv, xv, spread(mean[:, :], D), ALU.subtract).then_inc(ln_cent, 1)
                dve.wait_ge(ln_sq, n)
                dve.tensor_reduce(var[:, :], by_block(sq[:, :]), AX_X, ALU.add).then_inc(ln_var, 1)
                dve.wait_ge(ln_std, n)
                dve.reciprocal(rstd[:, :], std[:, :]).then_inc(ln_rstd, 1)
                dve.wait_ge(ln_rstd, n)
                dve.tensor_tensor(cv, cv, spread(rstd[:, :], D), ALU.mult).then_inc(ln_norm, 1)

            dve.wait_ge(consts_set, 8)
            dve.wait_ge(x_loaded, 16)
            layer_norm(1)

            dve.wait_ge(w2_turned, 1)
            dve.tensor_copy(w2bT[:, :], pair[3][0:D, 0, 0:D + 1]).then_inc(w2_kept, 1)
            dve.wait_ge(w2u_made, 1)
            dve.tensor_copy(w2u[:, :], pair[3][0:D + 1, 1, 0:D]).then_inc(w2u_kept, 1)

            def keep(k, to):
                h = k % 2
                g0, n = h * HALF[0], HALF[h]
                for q in range(2):
                    dve.wait_ge(key_turned, 2 * k + q + 1)
                    dve.tensor_copy(to[:, g0:g0 + n, 4 * q:4 * q + 4].rearrange("p g t -> p t g"),
                                    pair[3][:, q, :].rearrange("p (t g) -> p t g", g=P)[:, :, 0:n]).then_inc(key_kept, 1)

            dve.wait_ge(src_loaded, 48)
            for k in range(2):
                if k:
                    dve.wait_ge(key_turned, 2 * k)
                dve.tensor_copy(key_g[0:HALF[k], :], src_i[0:HALF[k], k, :]).then_inc(key_made, 1)
                keep(k, idx)

            dve.wait_ge(par_loaded, 16 * PARAMETERS)

            def chunk1(c, slot):
                wait_step(dve, hT_staged, c)
                dve.tensor_copy(hT[0:D, ds(c * CN, CN)], t_stage[:, slot, :]).then_inc(hT_kept, 1)
                wait_step(dve, t1_made, c)
                if not isinstance(c, int):
                    dve.wait_ge(t1_stored[slot], (c - slot) * 8)
                dve.tensor_tensor(by_block(row_stage[:, slot, :]), by_block(tall(slot)),
                                  b1_bc[:, :].rearrange("p (o f) -> p o f", o=1).to_broadcast([NP, BLK, D]),
                                  ALU.add).then_inc(t1_staged, 1)

            steps(dve, CHUNKS, 2, chunk1)

            dve.wait_ge(dst_loaded, 48)
            for h in range(2):
                n = HALF[h]
                dve.tensor_reduce(hi[0:n, h:h + 1], dst_i[0:n, h, :], AX_X, ALU.max).then_inc(range_made, 1)
                dve.tensor_reduce(lo[0:n, h:h + 1], dst_i[0:n, h, :], AX_X, ALU.min).then_inc(range_made, 1)
                dve.tensor_copy(base[0:n, h:h + 1], dst_i[0:n, h, 0:1]).then_inc(range_made, 1)
            dve.wait_ge(range_made, 6)
            for h in range(2):
                n = HALF[h]
                dve.scalar_tensor_tensor(out=above[0:n, h:h + 1], in0=hi[0:n, h:h + 1], scalar=1.0 - W,
                                         in1=base[0:n, h:h + 1], op0=ALU.add, op1=ALU.is_gt).then_inc(above_made, 1)
            dve.wait_ge(above_made, 2)
            for h in range(2):
                n = HALF[h]
                dve.scalar_tensor_tensor(out=bad[0:n, h:h + 1], in0=lo[0:n, h:h + 1], scalar=base[0:n, h:h + 1],
                                         in1=above[0:n, h:h + 1], op0=ALU.is_lt, op1=ALU.add).then_inc(bad_made, 1)
            dve.wait_ge(bad_summed, 1)
            dve.tensor_reduce(bad_all[:, :], pair[3][:, 0, 0:2], AX_X, ALU.add).then_inc(bad_counted, 1)
            dve.wait_ge(bad_counted, 1)
            dve.tensor_scalar(fast_f[:, :], bad_all[:, :], 0.5, None, ALU.is_lt).then_inc(fast_made, 1)
            dve.wait_ge(fast_made, 1)
            dve.tensor_copy(fast_i[:, :], fast_f[:, :]).then_inc(fast_made, 1)
            for h in range(2):
                dve.tensor_tensor(base[0:HALF[h], h:h + 1], base[0:HALF[h], h:h + 1], fast_f[0:HALF[h], :],
                                  ALU.mult).then_inc(range_made, 1)
            dve.wait_ge(base_turned, 2)
            for h in range(2):
                last = dve.tensor_copy(base_row[:, h * HALF[0]:h * HALF[0] + HALF[h]],
                                       pair[3][0:1, 1, h * P:h * P + HALF[h]])
            last.then_inc(base_made, 1)
            for k in range(2, 4):
                n = HALF[k - 2]
                dve.wait_ge(key_turned, 2 * k)
                made = dve.tensor_scalar(key_g[0:n, :], dst_i[0:n, k - 2, :], base[0:n, k - 2:k - 1], None, ALU.subtract)
                if k == 3:
                    made.then_inc(last_made, 1)
                    dve.wait_ge(last_made, 1)
                    dve.memset(key_g[n - 1:n, 0:OVERLAP], FAR).then_inc(key_made, 1)
                else:
                    made.then_inc(key_made, 1)
                keep(k, rel)
            dve.wait_ge(wgt_loaded, 48)
            for k in range(4, 6):
                keep(k, wgt)
            dve.memset(acc2, 0.0).then_inc(acc2_set, 1)
            dve.tensor_tensor(by_block(x_all[:, :]), by_block(x_all[:, :]),
                              c2_bc[:, :].rearrange("p (o f) -> p o f", o=1).to_broadcast([NP, NB, D]),
                              ALU.add).then_inc(c2_added, 1)
            dve.wait_ge(base_made, 1)
            dve.wait_ge(fast_made, 2)
            dve.wait_ge(consts_set, 8)
            dve.wait_ge(acc2_set, 1)
            fast = dve.value_load(fast_i[0:1, 0:1], min_val=0, max_val=1)

            iota_bc = iota[:, :].rearrange("p (o w) -> p o w", o=1).to_broadcast([P, T, W])

            def over_window(ap):
                return ap.rearrange("p (t o) -> p t o", o=1).to_broadcast([P, T, W])

            def at_group(table, g):
                return table[:, g, :] if isinstance(g, int) else table[:, ds(g, 1), :].rearrange("p o t -> p (o t)")

            def add_product(g, slot):
                gathered_wait(dve, g, slot, 0)
                wait_step(dve, q_made, g)
                wait_step(dve, hid_made, g - RING)
                dve.tensor_tensor(pre[:, slot, :, :], rows[:, slot, :, :],
                                  pair[slot][:, 1, :].rearrange("p (t f) -> p t f", f=D), ALU.add).then_inc(pre_made, 1)

            def accumulate(acc, m, start, n, done):
                to = acc[:, ds(start, W)]
                dve.tensor_tensor(to, to, pair[3][0:m, 0, 0:W], ALU.add).then_inc(done, 1)

            def fast1(g, slot):
                wait_step(dve, group_done, g - RING)
                dve.tensor_tensor(hot[:, slot, :, :], iota_bc, over_window(at_group(rel, g)),
                                  ALU.is_equal).then_inc(hot_made, 1)
                start = dve.value_load(base_row[0:1, ds(g, 1)], min_val=0, max_val=N)
                add_product(g, slot)
                wait_step(dve, group_done, g)
                wait_step(dve, acc_added, g - 1)
                accumulate(acc1, D + 1, start, g, acc_added)

            def fast2(g, slot):
                wait_step(dve, group_done, g - RING + GROUPS)
                dve.tensor_tensor(hot[:, slot, :, :], iota_bc, over_window(at_group(rel, g)),
                                  ALU.is_equal).then_inc(hot_made, 1)
                start = dve.value_load(base_row[0:1, ds(g, 1)], min_val=0, max_val=N)
                wait_step(dve, hot_made, g + GROUPS)
                dve.tensor_tensor(hot[:, slot, :, :], hot[:, slot, :, :], over_window(at_group(wgt, g)),
                                  ALU.mult).then_inc(hot_weighed, 1)
                wait_step(dve, group_done, g + GROUPS)
                wait_step(dve, acc_added, g + GROUPS - 1)
                accumulate(acc2, D, start, g, acc_added)

            def windows(acc, m, g, slot, done, weigh):
                n0 = (g + done) * WINDOWS
                dve.tensor_copy(key_now[:, slot, :], at_group(rel, g)).then_inc(key_moved, 1)
                moved0 = (g + done) * (WINDOWS + 1)
                with dve.Fori(0, WINDOWS) as k:
                    dve.wait_ge(key_moved, moved0 + k + 1)
                    dve.tensor_tensor(hot[:, slot, :, :], iota_bc, over_window(key_now[:, slot, :]),
                                      ALU.is_equal).then_inc(whot_made, 1)
                    dve.wait_ge(whot_made, n0 + k + 1)
                    if weigh:
                        dve.tensor_tensor(hot[:, slot, :, :], hot[:, slot, :, :], over_window(at_group(wgt, g)),
                                          ALU.mult).then_inc(whot_weighed, 1)
                    dve.tensor_scalar(key_now[:, slot, :], key_now[:, slot, :], -float(W), None,
                                      ALU.add).then_inc(key_moved, 1)
                    dve.wait_ge(wseg_made, n0 + k + 1)
                    accumulate(acc, m, k * W, None, wacc_added)
                    dve.wait_ge(wacc_added, n0 + k + 1)

            def slow1(g, slot):
                add_product(g, slot)
                windows(acc1, D + 1, g, slot, 0, False)
                dve.wait_ge(group_done, g + 1)

            def slow2(g, slot):
                windows(acc2, D, g, slot, GROUPS, True)
                dve.wait_ge(group_done, g + 1 + GROUPS)

            with dve.If(fast > 0):
                steps(dve, FULL, RING, fast1)
                fast1(FULL, 0)
                dve.wait_ge(acc_added, GROUPS)
            with dve.Else():
                steps(dve, FULL, RING, slow1)
                slow1(FULL, 0)
            dve.nop().then_inc(turn_made, 1)

            dve.wait_ge(c2_added, 1)

            def chunk2(c, slot):
                wait_step(dve, up_made, c)
                dve.tensor_tensor(chunked(x_all, c), chunked(x_all, c), tall(slot), ALU.add).then_inc(x1_made, 1)

            steps(dve, CHUNKS, 2, chunk2)
            dve.wait_ge(x1_made, CHUNKS)
            layer_norm(2)

            with dve.If(fast > 0):
                steps(dve, FULL, RING, fast2)
                fast2(FULL, 0)
                dve.wait_ge(acc_added, 2 * GROUPS)
            with dve.Else():
                steps(dve, FULL, RING, slow2)
                slow2(FULL, 0)
            dve.nop().then_inc(turn_made, 1)

            def chunk3(c, slot):
                wait_step(dve, a_turned, c)
                if not isinstance(c, int):
                    dve.wait_ge(out_stored[slot], (c - slot) * 8)
                dve.tensor_tensor(row_stage[:, slot, :], chunked(x_all, c), tall(slot),
                                  ALU.add).then_inc(out_staged, 1)

            steps(dve, CHUNKS, 2, chunk3)


_INS = ['x', 'src', 'dst', 'edge_attr_64', 'edge_weight', 'L0_gnn_W1', 'L0_gnn_b1', 'L0_gnn_W2', 'L0_gnn_b2',
        'L0_gnn_U1', 'L0_gnn_c1', 'L0_gnn_U2', 'L0_gnn_c2']


def kernel(**inputs):
    import numpy as _np
    import concourse.bacc as _bacc
    from concourse import mybir as _mybir
    from concourse.bass_utils import run_bass_kernel_spmd as _run

    nc = _bacc.Bacc("TRN2", target_bir_lowering=False, num_devices=1)
    arrays, args = {}, []
    for name in _INS:
        a = _np.ascontiguousarray(inputs[name])
        arrays[f"in_{name}_dram"] = a
        args.append(nc.dram_tensor(f"in_{name}_dram", a.shape, _mybir.dt.from_np(a.dtype), kind="ExternalInput").ap())
    shape = _np.asarray(inputs['x']).shape
    args.append(nc.dram_tensor("out_0_dram", shape, _mybir.dt.float32, kind="ExternalOutput").ap())
    build(nc, *args)
    r = _run(nc, [arrays], core_ids=[0])
    return r.results[0]["out_0_dram"]
```

```python
from contextlib import ExitStack

import concourse.bass as bass
from concourse import mybir

ALU = mybir.AluOpType
ACT = mybir.ActivationFunctionType
F32 = mybir.dt.float32
I32 = mybir.dt.int32
BF16 = mybir.dt.bfloat16
F16 = mybir.dt.float16
AX_X = mybir.AxisListType.X
AX_XY = mybir.AxisListType.XY
ds = bass.ds

P = 128
D = 64
T = 8
GE = P * T
W = 40
RING = 3
NP = 125
BLK = 5
CN = NP * BLK
BC = BLK * D
WT = 7
BATCH = RING * T
DRING = 8
PAIRS = BATCH // 2
PARTS = 3
FAR = -20000.0


def steps(eng, count, unroll, body):
    assert count % unroll == 0
    for slot in range(unroll):
        body(slot, slot)
    with eng.Fori(1, count // unroll) as turn:
        for slot in range(unroll):
            body(turn * unroll + slot, slot)


def wait_step(eng, sem, g, each=1):
    if not isinstance(g, int) or g >= 0:
        eng.wait_ge(sem, (g + 1) * each)


def build(nc, x, src, dst, edge_attr, edge_weight, w1, b1, w2, b2, u1, c1, u2, c2, out):
    N = x.shape[0]
    E = src.shape[0]
    NB = N // NP
    CHUNKS = NB // BLK
    FULL = E // GE
    GROUPS = FULL + 1
    OVERLAP = FULL * GE - (E - GE)
    BATCHES = 32
    HALF = (GROUPS - RING * BATCHES, RING * BATCHES)
    NHI = -(-N // P)
    NLAST = N - (NHI - 1) * P
    PARAMETERS = 11
    WINDOWS = -(-N // W)
    assert HALF[0] % RING == 1
    assert N == NB * NP and NB == CHUNKS * BLK and CHUNKS % 2 == 0 and FULL % RING == 0

    table1 = nc.dram_tensor("table1", (N, D), F32, kind="Internal").ap()
    table2 = nc.dram_tensor("table2", (N, D), F32, kind="Internal").ap()

    with ExitStack() as ctx:
        def sb(name, shape, dt=F32):
            return ctx.enter_context(nc.sbuf_tensor(name, shape, dt))

        def psum(name, shape):
            return ctx.enter_context(nc.psum_tensor(name, shape, F32))

        def sem(name):
            return ctx.enter_context(nc.semaphore(name))

        x_all = sb("x_all", [NP, NB * D])
        mid = sb("mid", [P, NB * D])
        cent = mid[0:NP, :]
        h2 = mid[:, 0:(NHI - 1) * D].rearrange("p (h f) -> p h f", f=D)
        h2_last = sb("h2_last", [P, D])
        row_sum = sb("row_sum", [NP, NB])
        mean = sb("mean", [NP, NB])
        var = sb("var", [NP, NB])
        std = sb("std", [NP, NB])
        rstd = sb("rstd", [NP, NB])
        stages = sb("stages", [P, 4 * BC])
        h_stage = stages[0:NP, 0:2 * BC].rearrange("p (s f) -> p s f", s=2)
        row_stage = stages[0:NP, 2 * BC:].rearrange("p (s f) -> p s f", s=2)
        nodes = sb("nodes", [P, 2 * N + W])
        node_cols = nodes[:, 0:N]
        hT = node_cols[0:D + 1, :]
        sq = node_cols[0:NP, 0:NB * D]
        acc1 = nodes[0:D + 1, N:]
        late = sb("late", [P, N + W])
        acc2 = late[0:D, :]
        t_stage = sb("t_stage", [D, 2, CN])
        early = late[:, 0:6 * GE].rearrange("g (k h e) -> g k h e", k=3, h=2)
        wgt_g = early[:, 0]
        dst_i = early[:, 1].bitcast(I32)
        src_i = early[:, 2].bitcast(I32)
        key_g = sb("key_g", [P, GE])
        hi = sb("hi", [P, 2])
        lo = sb("lo", [P, 2])
        base = sb("base", [P, 2])
        bad = sb("bad", [P, 3])
        above = sb("above", [P, 2])
        bad_all = sb("bad_all", [P, 1])
        fast_f = sb("fast_f", [P, 1])
        fast_i = sb("fast_i", [P, 1], I32)
        base_row = sb("base_row", [1, GROUPS], I32)
        rel = sb("rel", [P, GROUPS, T])
        idx = sb("idx", [P, GROUPS + RING, T], I32)
        wgt = sb("wgt", [P, GROUPS, T])
        idx_ring = sb("idx_ring", [P, RING, T], I32)
        rings = sb("rings", [P, NHI * BATCH * WT])
        ea_ring = rings[:, 0:RING * T * D].rearrange("p (s f) -> p s f", s=RING)
        eaT = rings[:, RING * T * D:2 * RING * T * D].rearrange("p (s a e) -> p s a e", s=RING, e=P)
        pre = rings[:, 2 * RING * T * D:3 * RING * T * D].rearrange("p (s t f) -> p s t f", s=RING, f=D)
        hid_end = 3 * RING * T * D + RING * T * (D + 1)
        hid = rings[:, 3 * RING * T * D:hid_end].rearrange("p (s t f) -> p s t f", s=RING, f=D + 1)
        rows = sb("rows", [P, RING, T, D])
        adjacency = [nodes[:, 0:NHI * BATCH * WT].rearrange("p (h c) -> p h c", h=NHI),
                     rings[:, :].rearrange("p (h c) -> p h c", h=NHI)]
        d_key = rings[0:HALF[1], hid_end:hid_end + GE]
        d_hi = rings[0:HALF[1], hid_end + GE:hid_end + 2 * GE].bitcast(I32)
        assert hid_end + 2 * GE <= NHI * BATCH * WT
        t_base = sb("t_base", [HALF[1], T])
        t_hi = sb("t_hi", [HALF[1], 1])
        t_lo = sb("t_lo", [HALF[1], 1])
        t_above = sb("t_above", [HALF[1], 1])
        tile_row = sb("tile_row", [1, HALF[1], T], I32)
        tile_tab = sb("tile_tab", [P, 2 + PARTS, T, HALF[1] + 1])
        tile_key = tile_tab[:, 0, :, 0:HALF[1]]
        tile_lo = tile_tab[:, 1, :, 0:HALF[1]]
        tile_w = tile_tab[:, 2:, :, 0:HALF[1]]
        key_bf = key_g[:, :].bitcast(BF16)
        tile_wb = key_bf[:, 0:T * HALF[1]].rearrange("p (t g) -> p t g", t=T)
        tile_now = sb("tile_now", [P, RING, 2 + PARTS, T])
        hot_key = sb("hot_key", [P, DRING, NHI * WT], BF16)
        hot_eq = key_bf[:, 0:DRING * P].rearrange("p (s e) -> p s e", s=DRING)
        hot_w0 = key_bf[:, DRING * P:2 * DRING * P].rearrange("p (s e) -> p s e", s=DRING)
        hot_w12 = stages[:, :].bitcast(BF16)[:, 0:2 * DRING * P].rearrange("p (s k e) -> p s k e", s=DRING, k=2)
        iota_key = sb("iota_key", [P, NHI * WT], F16)
        hot = sb("hot", [P, RING, T, W])
        key_now = sb("key_now", [P, RING, T])
        ident = sb("ident", [P, P])
        ones = sb("ones", [P, P])
        iota = sb("iota", [P, W])
        eps = sb("eps", [P, 1])
        w1a = sb("w1a", [D, D])
        w1b2 = sb("w1b2", [P, P])
        w2b = sb("w2b", [D + 1, D])
        w2bT = sb("w2bT", [D, D + 1])
        w2u = sb("w2u", [D + 1, D])
        u1a = sb("u1a", [D + 1, D])
        u1b = sb("u1b", [D, D])
        u2_s = sb("u2_s", [D, D])
        b1_bc = sb("b1_bc", [NP, D])
        c2_bc = sb("c2_bc", [NP, D])

        pair = [psum(f"pair{i}", [P, 2, 512]) for i in range(4)]

        def wide(slot):
            return pair[slot][0:D, :, :].rearrange("f b n -> f (b n)")[:, 0:BLK * P].rearrange(
                "f (b n) -> f b n", n=P)

        def tall(slot):
            return pair[2][0:NP, slot, 0:BC]

        x_loaded = sem("x_loaded")
        src_loaded = sem("src_loaded")
        dst_loaded = sem("dst_loaded")
        wgt_loaded = sem("wgt_loaded")
        par_loaded = sem("par_loaded")
        consts_set = sem("consts_set")
        t_base_made = sem("t_base_made")
        t_rel_made = sem("t_rel_made")
        t_range_made = sem("t_range_made")
        t_above_made = sem("t_above_made")
        t_hi_made = sem("t_hi_made")
        t_lo_made = sem("t_lo_made")
        w_split = sem("w_split")
        h2_loaded = sem("h2_loaded")
        columns_staged = sem("columns_staged")
        pair_hot = sem("pair_hot")
        pair_made = sem("pair_made")
        pair_kept = sem("pair_kept")
        tile_added = sem("tile_added")
        batch_added = sem("batch_added")
        pair_scaled = sem("pair_scaled")
        applied = sem("applied")
        pool_step = sem("pool_step")
        pe_held = sem("pe_held")
        pool_held = sem("pool_held")
        ones_set = sem("ones_set")
        key_made = sem("key_made")
        key_turned = sem("key_turned")
        key_kept = sem("key_kept")
        range_made = sem("range_made")
        bad_made = sem("bad_made")
        bad_summed = sem("bad_summed")
        fast_made = sem("fast_made")
        base_turned = sem("base_turned")
        base_made = sem("base_made")
        w2_turned = sem("w2_turned")
        w2_kept = sem("w2_kept")
        w2u_made = sem("w2u_made")
        w2u_kept = sem("w2u_kept")
        ln_sum = sem("ln_sum")
        ln_mean = sem("ln_mean")
        ln_cent = sem("ln_cent")
        ln_sq = sem("ln_sq")
        ln_var = sem("ln_var")
        ln_std = sem("ln_std")
        ln_rstd = sem("ln_rstd")
        ln_norm = sem("ln_norm")
        h_staged = sem("h_staged")
        h_turned = sem("h_turned")
        hT_staged = sem("hT_staged")
        hT_kept = sem("hT_kept")
        t1_made = sem("t1_made")
        t1_staged = sem("t1_staged")
        t1_stored = [sem(f"t1_stored{s}") for s in range(2)]
        c2_added = sem("c2_added")
        idx_ready = sem("idx_ready")
        gathered = [sem(f"gathered{s}") for s in range(RING)]
        ea_loaded = [sem(f"ea_loaded{s}") for s in range(RING)]
        ea_turned = sem("ea_turned")
        eaT_kept = sem("eaT_kept")
        q_made = sem("q_made")
        pre_made = sem("pre_made")
        hid_made = sem("hid_made")
        hot_made = sem("hot_made")
        hot_weighed = sem("hot_weighed")
        seg_made = sem("seg_made")
        acc_added = sem("acc_added")
        turn_made = sem("turn_made")
        group_done = sem("group_done")
        above_made = sem("above_made")
        bad_counted = sem("bad_counted")
        last_made = sem("last_made")
        key_moved = sem("key_moved")
        whot_made = sem("whot_made")
        whot_weighed = sem("whot_weighed")
        wseg_made = sem("wseg_made")
        wacc_added = sem("wacc_added")
        g_made = sem("g_made")
        g_staged = sem("g_staged")
        up_made = sem("up_made")
        x1_made = sem("x1_made")
        h2_staged = sem("h2_staged")
        t2_stored = [sem(f"t2_stored{s}") for s in range(2)]
        a_staged = sem("a_staged")
        a_turned = sem("a_turned")
        out_staged = sem("out_staged")
        out_stored = [sem(f"out_stored{s}") for s in range(2)]

        def build_banks(r):
            return pair[r % 2][:, :, 0:NHI * WT]

        def blocks(dram, c):
            return dram[ds(c * CN, CN), :].rearrange("(b p) f -> p b f", p=NP)

        def chunked(t, c):
            return t[:, ds(c * BC, BC)]

        def by_block(ap):
            return ap.rearrange("p (b f) -> p b f", f=D)

        def spread(ap, n):
            return ap.rearrange("p (b o) -> p b o", o=1).to_broadcast([ap.shape[0], ap.shape[1], n])

        def edge_row(place):
            return E - GE if isinstance(place, int) and place == 0 else (place - 1) * GE

        def gathered_wait(eng, g, slot, before):
            turns = -(-(before - slot) // RING) if before else 0
            if isinstance(g, int):
                eng.wait_ge(gathered[slot], (g // RING + 1 + turns) * 16 * T)
            else:
                eng.wait_ge(gathered[slot], ((g - slot) // RING + 1 + turns) * 16 * T)

        def rest_of_half(eng, body):
            with eng.Fori(BATCHES, (HALF[0] - 1) // RING) as turn:
                for slot in range(RING):
                    body(turn * RING + slot, slot)
            body(HALF[0] - 1, 0)

        block = ctx.enter_context(nc.Block())

        @block.sync
        def _(sp):
            sp.dma_start(by_block(x_all[:, :]), x.rearrange("(b p) f -> p b f", p=NP)).then_inc(x_loaded, 16)

            def load_groups(tile, dram, loaded):
                sp.dma_start(tile[0:1, 0, :], dram[E - GE:E].rearrange("(o e) -> o e", o=1)).then_inc(loaded, 16)
                split = (HALF[0] - 1) * GE
                sp.dma_start(tile[1:HALF[0], 0, :],
                             dram[0:split].rearrange("(g e) -> g e", e=GE)).then_inc(loaded, 16)
                sp.dma_start(tile[0:HALF[1], 1, :],
                             dram[split:FULL * GE].rearrange("(g e) -> g e", e=GE)).then_inc(loaded, 16)

            load_groups(src_i, src, src_loaded)
            load_groups(dst_i, dst, dst_loaded)
            load_groups(wgt_g, edge_weight, wgt_loaded)

            def load_ea(g, slot):
                wait_step(sp, ea_turned, g - RING)
                rows_of = edge_attr[ds(edge_row(g), GE), :].rearrange("(p t) f -> p (t f)", t=T)
                sp.dma_start(ea_ring[:, slot, :], rows_of).then_inc(ea_loaded[slot], 16)

            def store_t1(c, slot):
                wait_step(sp, t1_staged, c)
                sp.dma_start(blocks(table1, c), by_block(row_stage[:, slot, :])).then_inc(t1_stored[slot], 16)

            steps(sp, CHUNKS, 2, store_t1)
            steps(sp, FULL, RING, load_ea)
            load_ea(FULL, 0)

            def store_t2(c, slot):
                wait_step(sp, h2_staged, c)
                sp.dma_start(blocks(table2, c), by_block(h_stage[:, slot, :])).then_inc(t2_stored[slot], 16)

            steps(sp, CHUNKS, 2, store_t2)
            for s in range(2):
                sp.wait_ge(t2_stored[s], 16 * CHUNKS // 2)
            sp.dma_start(h2, table2[0:(NHI - 1) * P, :].rearrange("(h p) f -> p h f", p=P)).then_inc(h2_loaded, 16)
            sp.dma_start(h2_last[0:NLAST, :], table2[(NHI - 1) * P:N, :]).then_inc(h2_loaded, 16)

            def store_out(c, slot):
                wait_step(sp, out_staged, c)
                sp.dma_start(blocks(out, c), by_block(row_stage[:, slot, :])).then_inc(out_stored[slot], 16)

            steps(sp, CHUNKS, 2, store_out)
            for s in range(2):
                sp.wait_ge(t1_stored[s], 16 * CHUNKS // 2)
                sp.wait_ge(t2_stored[s], 16 * CHUNKS // 2)
                sp.wait_ge(out_stored[s], 16 * CHUNKS // 2)

        @block.gpsimd
        def _(pool):
            pool.memset(eps[:, :], 1e-5).then_inc(consts_set, 1)
            pool.memset(ones[:, :], 1.0).then_inc(consts_set, 1)
            pool.memset(ident[:, :], 0.0).then_inc(pool_step, 1)
            pool.memset(w1b2[:, :], 0.0).then_inc(pool_step, 1)
            pool.wait_ge(pool_step, 2)
            pool.affine_select(out=ident[:, :], in_=ident[:, :], compare_op=ALU.not_equal, fill=1.0, base=0,
                               pattern=[[-1, P]], channel_multiplier=1).then_inc(consts_set, 1)
            pool.iota(iota[:, :], [[1, W]], base=0, channel_multiplier=0,
                      allow_small_or_imprecise_dtypes=True).then_inc(consts_set, 1)
            pool.memset(bad[:, :], 0.0).then_inc(consts_set, 1)
            for to, of in ((w1a[:, :], w1[0:D, :]), (w1b2[0:D, 0:D], w1[D:2 * D, :]),
                           (w1b2[D:P, D:P], w1[D:2 * D, :]), (w2b[0:D, :], w2),
                           (w2b[D:D + 1, :], b2.rearrange("(o f) -> o f", o=1)),
                           (u1a[0:D, :], u1[0:D, :]), (u1b[:, :], u1[D:2 * D, :]), (u2_s[:, :], u2),
                           (u1a[D:D + 1, :], c1.rearrange("(o f) -> o f", o=1)),
                           (b1_bc[:, :], b1.rearrange("(o f) -> o f", o=1).to_broadcast([NP, D])),
                           (c2_bc[:, :], c2.rearrange("(o f) -> o f", o=1).to_broadcast([NP, D]))):
                pool.dma_start(to, of).then_inc(par_loaded, 16)
            pool.iota(iota_key[:, :], [[1, NHI * WT]], base=0, channel_multiplier=0,
                      allow_small_or_imprecise_dtypes=True).then_inc(consts_set, 1)
            pool.memset(h2_last[:, :], 0.0).then_inc(consts_set, 1)
            pool.memset(hid[:, :, :, D:D + 1], 1.0).then_inc(consts_set, 1)
            pool.memset(idx[:, GROUPS:, :], 0).then_inc(consts_set, 1)
            pool.memset(tile_tab[:, :, :, HALF[1]:], 0.0).then_inc(consts_set, 1)
            pool.memset(acc1[:, :], 0.0).then_inc(consts_set, 1)

            def gather(table, g, slot, used, before, refills):
                wait_step(pool, idx_ready, g + refills)
                wait_step(pool, used, g - RING + before)
                pool.sem_inc(pool_held, 1)
                for t in range(T):
                    pool.indirect_dma_start(
                        out=rows[:, slot, t, :], out_offset=None, in_=table,
                        in_offset=bass.IndirectOffsetOnAxis(ap=idx_ring[:, slot, t:t + 1], axis=0),
                    ).then_inc(gathered[slot], 16)

            pool.wait_ge(ln_var, 1)
            pool.memset(hT[D:D + 1, :], 1.0).then_inc(ones_set, 1)
            for s in range(2):
                pool.wait_ge(t1_stored[s], 16 * CHUNKS // 2)
            steps(pool, FULL, RING, lambda g, slot: gather(table1, g, slot, pre_made, 0, 0))
            gather(table1, FULL, 0, pre_made, 0, 0)
            pool.wait_ge(pre_made, GROUPS)
            for s in range(2):
                pool.wait_ge(t2_stored[s], 16 * CHUNKS // 2)
            def gather2(g, slot):
                gather(table2, g, slot, group_done, GROUPS, GROUPS + RING)

            pool.wait_ge(fast_made, 2)
            fast = pool.value_load(fast_i[0:1, 0:1], min_val=0, max_val=1)
            with pool.If(fast > 0):
                steps(pool, HALF[0] - 1, RING, gather2)
                gather2(HALF[0] - 1, 0)
            with pool.Else():
                steps(pool, FULL, RING, gather2)
                gather2(FULL, 0)

        @block.scalar
        def _(act):
            def layer_norm(n):
                act.wait_ge(ln_cent, n)
                act.activation(sq[:, :], cent[:, :], ACT.Square).then_inc(ln_sq, 1)
                act.wait_ge(ln_var, n)
                act.activation(std[:, :], var[:, :], ACT.Sqrt, bias=eps[0:NP, :], scale=1.0 / D).then_inc(ln_std, 1)
                act.wait_ge(ln_norm, n)

            def refill_idx(g, slot):
                act.copy(idx_ring[:, slot, :], idx[:, ds(g, 1), :].rearrange("p o t -> p (o t)")
                         if not isinstance(g, int) else idx[:, g, :]).then_inc(idx_ready, 1)

            act.wait_ge(consts_set, 1)
            layer_norm(1)

            def stage_h(c, slot):
                wait_step(act, h_turned, c - 2)
                act.activation(h_stage[:, slot, :], chunked(cent, c), ACT.Relu).then_inc(h_staged, 1)
                wait_step(act, h_turned, c)
                wait_step(act, t1_made, c - 2)
                wait_step(act, hT_kept, c - 2)
                act.copy(t_stage[:, slot, :].rearrange("f (b n) -> f b n", n=NP),
                         wide(slot)[:, :, 0:NP]).then_inc(hT_staged, 1)

            steps(act, CHUNKS, 2, stage_h)

            act.wait_ge(consts_set, 11)
            act.wait_ge(key_kept, 4)
            for s in range(RING):
                refill_idx(s, s)

            def pass1(g, slot):
                wait_step(act, ea_turned, g)
                wait_step(act, q_made, g - RING)
                act.copy(eaT[:, slot, :, :].rearrange("p a e -> p (a e)"), pair[slot][:, 0, :]).then_inc(eaT_kept, 1)
                wait_step(act, pre_made, g)
                wait_step(act, group_done, g - RING)
                act.activation(hid[:, slot, :, 0:D], pre[:, slot, :, :], ACT.Relu).then_inc(hid_made, 1)
                refill_idx(g + RING, slot)

            steps(act, FULL, RING, pass1)
            pass1(FULL, 0)

            def stage_g(c, slot):
                wait_step(act, g_made, c)
                wait_step(act, up_made, c - 2)
                act.activation(t_stage[:, slot, :].rearrange("f (b n) -> f b n", n=NP), wide(slot)[:, :, 0:NP],
                               ACT.Relu).then_inc(g_staged, 1)

            steps(act, CHUNKS, 2, stage_g)
            layer_norm(2)

            def stage_h2(c, slot):
                if not isinstance(c, int):
                    act.wait_ge(t2_stored[slot], (c - slot) * 8)
                act.activation(h_stage[:, slot, :], chunked(cent, c), ACT.Relu).then_inc(h2_staged, 1)

            steps(act, CHUNKS, 2, stage_h2)

            for s in range(RING):
                refill_idx(s, s)

            def pass2(g, slot):
                wait_step(act, group_done, g + GROUPS)
                refill_idx(g + RING, slot)

            def scale_pair(u, p, r):
                act.wait_ge(pair_hot, r + 1)
                for t in (2 * p, 2 * p + 1):
                    for k in range(2):
                        last = act.activation(hot_w12[:, t, k, :], hot_eq[:, t, :], ACT.Copy,
                                              scale=tile_now[:, u, 3 + k, t:t + 1])
                last.then_inc(pair_scaled, 1)

            def dense_turn(j, b):
                if not isinstance(j, int) or j >= 2:
                    act.wait_ge(applied, j - 1)
                for u in range(RING):
                    for p in range(T // 2):
                        n = u * (T // 2) + p
                        r = j * PAIRS + n
                        if not isinstance(j, int) or r + 1 < BATCHES * PAIRS:
                            scale_pair((n + 1) // (T // 2) % RING, (n + 1) % (T // 2), r + 1)
                        act.wait_ge(pair_made, r + 1)
                        act.copy(adjacency[b][:, :, n * 2 * WT:(n + 1) * 2 * WT].rearrange("p h (t w) -> p t h w", t=2),
                                 build_banks(n).rearrange("p t (h w) -> p t h w", w=WT)).then_inc(pair_kept, 1)
                        if p == 1 and (u or not isinstance(j, int) or j):
                            pass2(j * RING + u - 1, (u - 1) % RING)

            act.wait_ge(fast_made, 2)
            fast = act.value_load(fast_i[0:1, 0:1], min_val=0, max_val=1)
            with act.If(fast > 0):
                for s in range(2):
                    act.wait_ge(t1_stored[s], 16 * CHUNKS // 2)
                    act.wait_ge(t2_stored[s], 16 * CHUNKS // 2)
                scale_pair(0, 0, 0)
                steps(act, BATCHES - 2, 2, dense_turn)
                dense_turn(BATCHES - 2, 0)
                dense_turn(BATCHES - 1, 1)
                pass2(RING * BATCHES - 1, RING - 1)
                rest_of_half(act, pass2)
            with act.Else():
                steps(act, FULL, RING, pass2)
                pass2(FULL, 0)
            act.wait_ge(turn_made, 2)

            def stage_a(c, slot):
                wait_step(act, a_turned, c - 2)
                act.copy(t_stage[:, slot, :], acc2[:, ds(c * CN, CN)]).then_inc(a_staged, 1)

            steps(act, CHUNKS, 2, stage_a)

        @block.tensor
        def _(pe):
            def hold():
                pe.sem_inc(pe_held, 1)

            pe.wait_ge(consts_set, 5)
            pe.wait_ge(par_loaded, 16 * PARAMETERS)

            pe.transpose(pair[3][0:D, 0, 0:D + 1], w2b[:, :], ident[0:D + 1, 0:D + 1]).then_inc(w2_turned, 1)
            pe.wait_ge(w2_kept, 1)
            pe.matmul(pair[3][0:D + 1, 1, 0:D], w2bT[:, :], u1b[:, :], start=True, stop=True).then_inc(w2u_made, 1)
            pe.wait_ge(w2u_kept, 1)

            def turn(k):
                h = k % 2 if k < 6 else 1
                n = HALF[h]
                if k not in (4, 5, 8, 9):
                    pe.wait_ge(key_made, k + 1 if k < 4 else k - 1)
                for q in range(2):
                    if 2 * k + q >= 2:
                        pe.wait_ge(key_kept, 2 * k + q - 1)
                    for t in range(4 * q, 4 * q + 4):
                        if k < 6:
                            of = key_g[0:n, :] if k < 4 else wgt_g[0:n, h, :]
                            of = of.rearrange("g (p t) -> g t p", t=T)[:, t, :]
                        elif k < 9:
                            of = (d_key, key_g[0:n, :], wgt_g[0:n, 1, :])[k - 6][:, t * P:(t + 1) * P]
                        else:
                            of = t_base[:, t:t + 1]
                        last = pe.transpose(pair[3][0:of.shape[1], q, (t % 4) * P:(t % 4) * P + n], of, ident[0:n, 0:n])
                    last.then_inc(key_turned, 1)

            for k in range(2):
                turn(k)

            def chunk1(c, slot):
                wait_step(pe, h_staged, c)
                wait_step(pe, hT_staged, c - 2)
                hold()
                for b in range(BLK):
                    last = pe.transpose(wide(slot)[:, b, 0:NP], h_stage[:, slot, b * D:(b + 1) * D],
                                        ident[0:NP, 0:NP])
                last.then_inc(h_turned, 1)
                wait_step(pe, hT_staged, c)
                wait_step(pe, t1_staged, c - 2)
                for b in range(BLK):
                    last = pe.matmul(tall(slot)[:, b * D:(b + 1) * D], t_stage[:, slot, b * NP:(b + 1) * NP],
                                     w1a[:, :], start=True, stop=True)
                last.then_inc(t1_made, 1)

            steps(pe, CHUNKS, 2, chunk1)

            pe.wait_ge(key_kept, 4)
            pe.wait_ge(bad_made, 3)
            pe.matmul(pair[3][:, 0, 0:3], ones[:, :], bad[:, :], start=True, stop=True).then_inc(bad_summed, 1)
            for h in range(2):
                pe.wait_ge(range_made, 3 * 2 + 1 + h)
                pe.transpose(pair[3][0:1, 1, h * P:h * P + HALF[h]], base[0:HALF[h], h:h + 1],
                             ident[0:HALF[h], 0:HALF[h]]).then_inc(base_turned, 1)
            pe.wait_ge(base_made, 1)
            for k in range(2, 4):
                turn(k)
            pe.wait_ge(wgt_loaded, 48)
            for k in range(4, 6):
                turn(k)
            for k in range(6, 10):
                turn(k)
            pe.wait_ge(key_kept, 20)
            pe.wait_ge(consts_set, 11)

            pe.wait_ge(fast_made, 2)
            fast = pe.value_load(fast_i[0:1, 0:1], min_val=0, max_val=1)

            def products(g, slot):
                pe.wait_ge(ea_loaded[slot], g // RING * 16 + 16) if isinstance(g, int) else \
                    pe.wait_ge(ea_loaded[slot], (g - slot) // RING * 16 + 16)
                wait_step(pe, eaT_kept, g - RING)
                for a in range(T // 2):
                    last = pe.transpose(pair[slot][:, 0, a * P:(a + 1) * P],
                                        ea_ring[:, slot, a * P:(a + 1) * P], ident[:, :])
                last.then_inc(ea_turned, 1)
                wait_step(pe, eaT_kept, g)
                wait_step(pe, pre_made, g - RING)
                for a in range(T // 2):
                    last = pe.matmul(pair[slot][:, 1, a * P:(a + 1) * P], eaT[:, slot, a, :], w1b2[:, :],
                                     start=True, stop=True)
                last.then_inc(q_made, 1)

            def segment(lhs, slot, bank, m):
                for t in range(T):
                    last = pe.matmul(pair[3][0:m, bank, 0:W], lhs[:, slot, t, 0:m], hot[:, slot, t, :],
                                     start=(t == 0), stop=(t == T - 1))
                return last

            def fast1(g, slot):
                products(g, slot)
                wait_step(pe, hot_made, g)
                wait_step(pe, hid_made, g)
                wait_step(pe, acc_added, g - 1)
                segment(hid, slot, 0, D + 1).then_inc(group_done, 1)

            def segment2(g, slot, bank):
                wait_step(pe, hot_weighed, g)
                gathered_wait(pe, g, slot, GROUPS)
                segment(rows, slot, bank, D).then_inc(group_done, 1)

            def apply(b, low, high):
                for hi in range(low, high):
                    of = h2_last[:, :] if hi == NHI - 1 else h2[:, hi, :]
                    last = pe.matmul(pair[2][0:D, b % 2, 0:BATCH * WT], of, adjacency[b % 2][:, hi, :],
                                     start=(hi == 0), stop=(hi == NHI - 1))
                return last

            def dense_turn(j, b):
                first = isinstance(j, int) and j == 0
                for u in range(RING):
                    for p in range(T // 2):
                        n = u * (T // 2) + p
                        r = j * PAIRS + n
                        pe.wait_ge(pair_scaled, r + 1)
                        wait_step(pe, pair_kept, r - 2)
                        for t in (2 * p, 2 * p + 1):
                            for k in range(PARTS):
                                lo = hot_w12[:, t, k - 1, :] if k else hot_w0[:, t, :]
                                last = pe.matmul(build_banks(n)[:, t % 2, :], lo, hot_key[:, t, :],
                                                 start=(k == 0), stop=(k == PARTS - 1))
                        last.then_inc(pair_made, 1)
                        if not first:
                            if n == 0:
                                pe.wait_ge(pair_kept, j * PAIRS)
                                if isinstance(j, int):
                                    pe.wait_ge(h2_loaded, 32)
                                else:
                                    pe.wait_ge(batch_added, j - 1)
                            low = 4 * n
                            last = apply(1 - b, low, NHI if n == PAIRS - 1 else low + 4)
                            if n == PAIRS - 1:
                                last.then_inc(applied, 1)
                    wait_step(pe, acc_added, j * RING + u - 2 + GROUPS)
                    segment2(j * RING + u, u, (b * RING + u) % 2)

            def slow1(g, slot):
                products(g, slot)
                wait_step(pe, hid_made, g)
                windows(lambda: segment(hid, slot, 0, D + 1), whot_made, g, g)

            def slow2(g, slot):
                gathered_wait(pe, g, slot, GROUPS)
                windows(lambda: segment(rows, slot, 0, D), whot_weighed, g, g + GROUPS)

            def windows(product, made, g_made, g_done):
                hold()
                with pe.Fori(0, WINDOWS) as k:
                    pe.wait_ge(made, g_made * WINDOWS + k + 1)
                    product().then_inc(wseg_made, 1)
                    pe.wait_ge(wacc_added, g_done * WINDOWS + k + 1)
                pe.nop().then_inc(group_done, 1)

            with pe.If(fast > 0):
                steps(pe, FULL, RING, fast1)
                fast1(FULL, 0)
            with pe.Else():
                steps(pe, FULL, RING, slow1)
                slow1(FULL, 0)

            pe.wait_ge(turn_made, 1)
            pe.wait_ge(ones_set, 1)
            def chunk2(c, slot):
                wait_step(pe, g_staged, c - 2)
                for b0, nb in ((0, 4), (4, 1)):
                    to = wide(slot)[:, b0:b0 + nb, 0:NP]
                    pe.matmul(to, u1a[:, :], hT[:, ds(c * CN + b0 * NP, nb * NP)].rearrange("f (b n) -> f b n", n=NP),
                              start=True, stop=False)
                    last = pe.matmul(to, w2u[:, :],
                                     acc1[:, ds(c * CN + b0 * NP, nb * NP)].rearrange("f (b n) -> f b n", n=NP),
                                     start=False, stop=True)
                last.then_inc(g_made, 1)
                wait_step(pe, g_staged, c)
                wait_step(pe, x1_made, c - 2)
                for b in range(BLK):
                    last = pe.matmul(tall(slot)[:, b * D:(b + 1) * D], t_stage[:, slot, b * NP:(b + 1) * NP],
                                     u2_s[:, :], start=True, stop=True)
                last.then_inc(up_made, 1)

            steps(pe, CHUNKS, 2, chunk2)

            pe.wait_ge(x1_made, CHUNKS)
            with pe.If(fast > 0):
                steps(pe, BATCHES, 2, dense_turn)
                pe.wait_ge(pair_kept, BATCHES * PAIRS)
                pe.wait_ge(batch_added, BATCHES - 1)
                apply(BATCHES - 1, 0, NHI).then_inc(applied, 1)

                def rest(g, slot):
                    pe.wait_ge(acc_added, g + GROUPS)
                    segment2(g, slot, 0)

                rest_of_half(pe, rest)
            with pe.Else():
                steps(pe, FULL, RING, slow2)
                slow2(FULL, 0)

            def chunk3(c, slot):
                wait_step(pe, a_staged, c)
                wait_step(pe, out_staged, c - 2)
                hold()
                for b in range(BLK):
                    last = pe.transpose(tall(slot)[:, b * D:(b + 1) * D], t_stage[:, slot, b * NP:(b + 1) * NP],
                                        ident[0:D, 0:D])
                last.then_inc(a_turned, 1)

            steps(pe, CHUNKS, 2, chunk3)

        @block.vector
        def _(dve):
            def layer_norm(n):
                xv, cv = by_block(x_all[:, :]), by_block(cent[:, :])
                dve.tensor_reduce(row_sum[:, :], xv, AX_X, ALU.add).then_inc(ln_sum, 1)
                dve.wait_ge(ln_sum, n)
                dve.tensor_scalar(mean[:, :], row_sum[:, :], 1.0 / D, None, ALU.mult).then_inc(ln_mean, 1)
                dve.wait_ge(ln_mean, n)
                dve.tensor_tensor(cv, xv, spread(mean[:, :], D), ALU.subtract).then_inc(ln_cent, 1)
                dve.wait_ge(ln_sq, n)
                dve.tensor_reduce(var[:, :], by_block(sq[:, :]), AX_X, ALU.add).then_inc(ln_var, 1)
                dve.wait_ge(ln_std, n)
                dve.reciprocal(rstd[:, :], std[:, :]).then_inc(ln_rstd, 1)
                dve.wait_ge(ln_rstd, n)
                dve.tensor_tensor(cv, cv, spread(rstd[:, :], D), ALU.mult).then_inc(ln_norm, 1)

            dve.wait_ge(consts_set, 11)
            dve.wait_ge(x_loaded, 16)
            layer_norm(1)

            dve.wait_ge(w2_turned, 1)
            dve.tensor_copy(w2bT[:, :], pair[3][0:D, 0, 0:D + 1]).then_inc(w2_kept, 1)
            dve.wait_ge(w2u_made, 1)
            dve.tensor_copy(w2u[:, :], pair[3][0:D + 1, 1, 0:D]).then_inc(w2u_kept, 1)

            def keep(k, to):
                h = k % 2
                g0, n = h * HALF[0], HALF[h]
                for q in range(2):
                    dve.wait_ge(key_turned, 2 * k + q + 1)
                    dve.tensor_copy(to[:, g0:g0 + n, 4 * q:4 * q + 4].rearrange("p g t -> p t g"),
                                    pair[3][:, q, :].rearrange("p (t g) -> p t g", g=P)[:, :, 0:n]).then_inc(key_kept, 1)

            dve.wait_ge(src_loaded, 48)
            for k in range(2):
                if k:
                    dve.wait_ge(key_turned, 2 * k)
                dve.tensor_copy(key_g[0:HALF[k], :], src_i[0:HALF[k], k, :]).then_inc(key_made, 1)
                keep(k, idx)

            dve.wait_ge(par_loaded, 16 * PARAMETERS)

            def chunk1(c, slot):
                wait_step(dve, hT_staged, c)
                dve.tensor_copy(hT[0:D, ds(c * CN, CN)], t_stage[:, slot, :]).then_inc(hT_kept, 1)
                wait_step(dve, t1_made, c)
                if not isinstance(c, int):
                    dve.wait_ge(t1_stored[slot], (c - slot) * 8)
                dve.tensor_tensor(by_block(row_stage[:, slot, :]), by_block(tall(slot)),
                                  b1_bc[:, :].rearrange("p (o f) -> p o f", o=1).to_broadcast([NP, BLK, D]),
                                  ALU.add).then_inc(t1_staged, 1)

            steps(dve, CHUNKS, 2, chunk1)

            dve.wait_ge(dst_loaded, 48)
            for h in range(2):
                n = HALF[h]
                dve.tensor_reduce(hi[0:n, h:h + 1], dst_i[0:n, h, :], AX_X, ALU.max).then_inc(range_made, 1)
                dve.tensor_reduce(lo[0:n, h:h + 1], dst_i[0:n, h, :], AX_X, ALU.min).then_inc(range_made, 1)
                dve.tensor_copy(base[0:n, h:h + 1], dst_i[0:n, h, 0:1]).then_inc(range_made, 1)
            dve.wait_ge(range_made, 6)
            for h in range(2):
                n = HALF[h]
                dve.scalar_tensor_tensor(out=above[0:n, h:h + 1], in0=hi[0:n, h:h + 1], scalar=1.0 - W,
                                         in1=base[0:n, h:h + 1], op0=ALU.add, op1=ALU.is_gt).then_inc(above_made, 1)
            dve.wait_ge(above_made, 2)
            for h in range(2):
                n = HALF[h]
                dve.scalar_tensor_tensor(out=bad[0:n, h:h + 1], in0=lo[0:n, h:h + 1], scalar=base[0:n, h:h + 1],
                                         in1=above[0:n, h:h + 1], op0=ALU.is_lt, op1=ALU.add).then_inc(bad_made, 1)
            n = HALF[1]

            def tiles(ap):
                return ap.rearrange("g (t e) -> g t e", t=T)

            dve.tensor_copy(t_base[:, :], tiles(dst_i[0:n, 1, :])[:, :, 0]).then_inc(t_base_made, 1)
            dve.wait_ge(t_base_made, 1)
            dve.tensor_tensor(tiles(d_key), tiles(dst_i[0:n, 1, :]),
                              t_base[:, :].rearrange("g (t o) -> g t o", o=1).to_broadcast([n, T, P]),
                              ALU.subtract).then_inc(t_rel_made, 1)
            dve.wait_ge(t_rel_made, 1)
            dve.tensor_reduce(t_hi[:, :], d_key, AX_X, ALU.max).then_inc(t_range_made, 1)
            dve.tensor_reduce(t_lo[:, :], d_key, AX_X, ALU.min).then_inc(t_range_made, 1)
            dve.wait_ge(t_range_made, 2)
            dve.tensor_scalar(t_above[:, :], t_hi[:, :], WT - 0.5, None, ALU.is_gt).then_inc(t_above_made, 1)
            dve.wait_ge(t_above_made, 1)
            dve.scalar_tensor_tensor(out=bad[0:n, 2:3], in0=t_lo[:, :], scalar=0.0, in1=t_above[:, :],
                                     op0=ALU.is_lt, op1=ALU.add).then_inc(bad_made, 1)
            dve.wait_ge(bad_summed, 1)
            dve.tensor_reduce(bad_all[:, :], pair[3][:, 0, 0:3], AX_X, ALU.add).then_inc(bad_counted, 1)
            dve.wait_ge(bad_counted, 1)
            dve.tensor_scalar(fast_f[:, :], bad_all[:, :], 0.5, None, ALU.is_lt).then_inc(fast_made, 1)
            dve.wait_ge(fast_made, 1)
            dve.tensor_copy(fast_i[:, :], fast_f[:, :]).then_inc(fast_made, 1)
            for h in range(2):
                dve.tensor_tensor(base[0:HALF[h], h:h + 1], base[0:HALF[h], h:h + 1], fast_f[0:HALF[h], :],
                                  ALU.mult).then_inc(range_made, 1)
            dve.wait_ge(base_turned, 2)
            for h in range(2):
                last = dve.tensor_copy(base_row[:, h * HALF[0]:h * HALF[0] + HALF[h]],
                                       pair[3][0:1, 1, h * P:h * P + HALF[h]])
            last.then_inc(base_made, 1)
            for k in range(2, 4):
                n = HALF[k - 2]
                dve.wait_ge(key_turned, 2 * k)
                made = dve.tensor_scalar(key_g[0:n, :], dst_i[0:n, k - 2, :], base[0:n, k - 2:k - 1], None, ALU.subtract)
                if k == 2:
                    made.then_inc(last_made, 1)
                    dve.wait_ge(last_made, 1)
                    dve.memset(key_g[0:1, 0:OVERLAP], FAR).then_inc(key_made, 1)
                else:
                    made.then_inc(key_made, 1)
                keep(k, rel)
            dve.wait_ge(wgt_loaded, 48)
            for k in range(4, 6):
                keep(k, wgt)
            n = HALF[1]
            dve.tensor_scalar(d_hi, src_i[0:n, 1, :], 7, None, ALU.arith_shift_right).then_inc(t_hi_made, 1)
            dve.wait_ge(t_hi_made, 1)
            dve.scalar_tensor_tensor(out=d_key, in0=d_hi, scalar=float(WT), in1=d_key, op0=ALU.mult,
                                     op1=ALU.add).then_inc(key_made, 1)
            dve.wait_ge(key_made, 5)
            dve.tensor_scalar(d_hi, src_i[0:n, 1, :], P - 1, None, ALU.bitwise_and).then_inc(t_lo_made, 1)
            dve.wait_ge(t_lo_made, 1)
            dve.wait_ge(key_turned, 8)
            dve.tensor_copy(key_g[0:n, :], d_hi).then_inc(key_made, 1)

            def keep_tiles(k, to):
                for q in range(2):
                    dve.wait_ge(key_turned, 2 * k + q + 1)
                    dve.tensor_copy(to[:, 4 * q:4 * q + 4, :],
                                    pair[3][0:to.shape[0], q, :].rearrange("p (t g) -> p t g", g=P)[:, :, 0:n]
                                    ).then_inc(key_kept, 1)

            keep_tiles(6, tile_key)
            keep_tiles(7, tile_lo)
            keep_tiles(8, tile_w[:, 0, :, :])
            keep_tiles(9, tile_row[:, :, :].rearrange("o g t -> o t g"))
            dve.wait_ge(key_kept, 18)
            for k in range(PARTS - 1):
                if k:
                    dve.wait_ge(w_split, 3 * k)
                dve.tensor_copy(tile_wb, tile_w[:, k, :, :]).then_inc(w_split, 1)
                dve.wait_ge(w_split, 3 * k + 1)
                dve.tensor_tensor(tile_w[:, k + 1, :, :], tile_w[:, k, :, :], tile_wb,
                                  ALU.subtract).then_inc(w_split, 1)
                dve.wait_ge(w_split, 3 * k + 2)
                dve.tensor_copy(tile_w[:, k, :, :], tile_wb).then_inc(w_split, 1)
            dve.memset(acc2, 0.0).then_inc(batch_added, 1)
            dve.tensor_tensor(by_block(x_all[:, :]), by_block(x_all[:, :]),
                              c2_bc[:, :].rearrange("p (o f) -> p o f", o=1).to_broadcast([NP, NB, D]),
                              ALU.add).then_inc(c2_added, 1)
            dve.wait_ge(base_made, 1)
            dve.wait_ge(fast_made, 2)
            dve.wait_ge(consts_set, 11)
            dve.wait_ge(batch_added, 1)
            fast = dve.value_load(fast_i[0:1, 0:1], min_val=0, max_val=1)

            iota_bc = iota[:, :].rearrange("p (o w) -> p o w", o=1).to_broadcast([P, T, W])

            def over_window(ap):
                return ap.rearrange("p (t o) -> p t o", o=1).to_broadcast([P, T, W])

            def at_group(table, g):
                return table[:, g, :] if isinstance(g, int) else table[:, ds(g, 1), :].rearrange("p o t -> p (o t)")

            def add_product(g, slot):
                gathered_wait(dve, g, slot, 0)
                wait_step(dve, q_made, g)
                wait_step(dve, hid_made, g - RING)
                dve.tensor_tensor(pre[:, slot, :, :], rows[:, slot, :, :],
                                  pair[slot][:, 1, :].rearrange("p (t f) -> p t f", f=D), ALU.add).then_inc(pre_made, 1)

            def accumulate(acc, m, start, n, done):
                to = acc[:, ds(start, W)]
                dve.tensor_tensor(to, to, pair[3][0:m, 0, 0:W], ALU.add).then_inc(done, 1)

            def fast1(g, slot):
                wait_step(dve, group_done, g - RING)
                dve.tensor_tensor(hot[:, slot, :, :], iota_bc, over_window(at_group(rel, g)),
                                  ALU.is_equal).then_inc(hot_made, 1)
                start = dve.value_load(base_row[0:1, ds(g, 1)], min_val=0, max_val=N)
                add_product(g, slot)
                wait_step(dve, group_done, g)
                wait_step(dve, acc_added, g - 1)
                accumulate(acc1, D + 1, start, g, acc_added)

            def group_hot(g, slot):
                wait_step(dve, group_done, g - RING + GROUPS)
                dve.tensor_tensor(hot[:, slot, :, :], iota_bc, over_window(at_group(rel, g)),
                                  ALU.is_equal).then_inc(hot_made, 1)
                wait_step(dve, hot_made, g + GROUPS)
                dve.tensor_tensor(hot[:, slot, :, :], hot[:, slot, :, :], over_window(at_group(wgt, g)),
                                  ALU.mult).then_inc(hot_weighed, 1)

            def add_group(g, bank):
                start = dve.value_load(base_row[0:1, ds(g, 1)], min_val=0, max_val=N)
                wait_step(dve, group_done, g + GROUPS)
                wait_step(dve, acc_added, g - 1 + GROUPS)
                to = acc2[:, ds(start, W)]
                dve.tensor_tensor(to, to, pair[3][0:D, bank, 0:W], ALU.add).then_inc(acc_added, 1)

            def tile_bases(place):
                return nc.values_load_multi_w_load_instructions(
                    tile_row[0:1, ds(place, 1), :].rearrange("o g t -> o (g t)"),
                    engines=[mybir.EngineType.DVE], min_val=0, max_val=N,
                    skip_runtime_bounds_check_because="they are destination nodes, and acc2 is a window wider")[1]

            def add_tile(start, i, bank):
                if i:
                    dve.wait_ge(tile_added, i)
                to = acc2[:, ds(start, WT)]
                dve.tensor_tensor(to, to, pair[2][0:D, bank, i * WT:(i + 1) * WT], ALU.add).then_inc(tile_added, 1)

            def end_batch():
                dve.wait_ge(tile_added, BATCH)
                dve.sem_clear(tile_added)
                dve.sem_inc(batch_added, 1)

            def stage_columns(g, u):
                dve.tensor_copy(tile_now[:, u, :, :].rearrange("p k t -> p (k t)"),
                                tile_tab[:, :, :, ds(g, 1)].rearrange("p k t o -> p (k t o)")
                                ).then_inc(columns_staged, 1)

            def dense_turn(j, b):
                first = isinstance(j, int)
                for u in range(RING):
                    g = j * RING + u
                    group_hot(g, u)
                    dve.wait_ge(columns_staged, g + 1)
                    if not first:
                        starts = tile_bases(g - 2 * RING)
                    for t in range(T):
                        if t % 4 == 0:
                            made = j * PAIRS + (u * T + t) // 2 - 2
                            if not first or made > 0:
                                dve.wait_ge(pair_made, made)
                        key, lo, w0 = (tile_now[:, u, k, t:t + 1] for k in range(3))
                        dve.tensor_scalar(hot_key[:, t, :], iota_key[:, :], key, None, ALU.is_equal)
                        dve.tensor_scalar(hot_w0[:, t, :], iota_key[:, 0:P], lo, w0, ALU.is_equal, ALU.mult)
                        last = dve.tensor_scalar(hot_eq[:, t, :], iota_key[:, 0:P], lo, None, ALU.is_equal)
                        if t % 2 == 1:
                            last.then_inc(pair_hot, 1)
                        if not first:
                            if u == 0 and t == 0:
                                dve.wait_ge(applied, j - 1)
                            if t in (0, 4):
                                dve.wait_ge(acc_added, g - 1 + GROUPS + (t == 4))
                            add_tile(starts[t], u * T + t, b)
                        if t == 3 and not (first and j + u == 0):
                            if not first:
                                dve.wait_ge(tile_added, u * T + t + 1)
                            add_group(g - 1, (b + u + 1) % 2)
                        if t == 5:
                            stage_columns(g + 1, (u + 1) % RING)
                if not first:
                    end_batch()

            def add_batch(b):
                dve.wait_ge(applied, b + 1)
                for u in range(RING):
                    starts = tile_bases(b * RING + u)
                    for t in range(T):
                        add_tile(starts[t], u * T + t, b % 2)
                end_batch()

            def rest(g, slot):
                group_hot(g, slot)
                add_group(g, 0)

            def windows(acc, m, g, slot, done, weigh):
                n0 = (g + done) * WINDOWS
                dve.tensor_copy(key_now[:, slot, :], at_group(rel, g)).then_inc(key_moved, 1)
                moved0 = (g + done) * (WINDOWS + 1)
                with dve.Fori(0, WINDOWS) as k:
                    dve.wait_ge(key_moved, moved0 + k + 1)
                    dve.tensor_tensor(hot[:, slot, :, :], iota_bc, over_window(key_now[:, slot, :]),
                                      ALU.is_equal).then_inc(whot_made, 1)
                    dve.wait_ge(whot_made, n0 + k + 1)
                    if weigh:
                        dve.tensor_tensor(hot[:, slot, :, :], hot[:, slot, :, :], over_window(at_group(wgt, g)),
                                          ALU.mult).then_inc(whot_weighed, 1)
                    dve.tensor_scalar(key_now[:, slot, :], key_now[:, slot, :], -float(W), None,
                                      ALU.add).then_inc(key_moved, 1)
                    dve.wait_ge(wseg_made, n0 + k + 1)
                    accumulate(acc, m, k * W, None, wacc_added)
                    dve.wait_ge(wacc_added, n0 + k + 1)

            def slow1(g, slot):
                add_product(g, slot)
                windows(acc1, D + 1, g, slot, 0, False)
                dve.wait_ge(group_done, g + 1)

            def slow2(g, slot):
                windows(acc2, D, g, slot, GROUPS, True)
                dve.wait_ge(group_done, g + 1 + GROUPS)

            with dve.If(fast > 0):
                steps(dve, FULL, RING, fast1)
                fast1(FULL, 0)
                dve.wait_ge(acc_added, GROUPS)
            with dve.Else():
                steps(dve, FULL, RING, slow1)
                slow1(FULL, 0)
            dve.nop().then_inc(turn_made, 1)

            dve.wait_ge(c2_added, 1)

            def chunk2(c, slot):
                wait_step(dve, up_made, c)
                dve.tensor_tensor(chunked(x_all, c), chunked(x_all, c), tall(slot), ALU.add).then_inc(x1_made, 1)

            steps(dve, CHUNKS, 2, chunk2)
            dve.wait_ge(x1_made, CHUNKS)
            layer_norm(2)

            with dve.If(fast > 0):
                stage_columns(0, 0)
                steps(dve, BATCHES, 2, dense_turn)
                add_group(RING * BATCHES - 1, 1)
                dve.wait_ge(acc_added, RING * BATCHES + GROUPS)
                add_batch(BATCHES - 2)
                rest_of_half(dve, rest)
                dve.wait_ge(acc_added, HALF[0] + GROUPS)
                add_batch(BATCHES - 1)
            with dve.Else():
                steps(dve, FULL, RING, slow2)
                slow2(FULL, 0)
            dve.nop().then_inc(turn_made, 1)

            def chunk3(c, slot):
                wait_step(dve, a_turned, c)
                if not isinstance(c, int):
                    dve.wait_ge(out_stored[slot], (c - slot) * 8)
                dve.tensor_tensor(row_stage[:, slot, :], chunked(x_all, c), tall(slot),
                                  ALU.add).then_inc(out_staged, 1)

            steps(dve, CHUNKS, 2, chunk3)


_INS = ['x', 'src', 'dst', 'edge_attr_64', 'edge_weight', 'L0_gnn_W1', 'L0_gnn_b1', 'L0_gnn_W2', 'L0_gnn_b2',
        'L0_gnn_U1', 'L0_gnn_c1', 'L0_gnn_U2', 'L0_gnn_c2']


def kernel(**inputs):
    import numpy as _np
    import concourse.bacc as _bacc
    from concourse import mybir as _mybir
    from concourse.bass_utils import run_bass_kernel_spmd as _run

    nc = _bacc.Bacc("TRN2", target_bir_lowering=False, num_devices=1)
    arrays, args = {}, []
    for name in _INS:
        a = _np.ascontiguousarray(inputs[name])
        arrays[f"in_{name}_dram"] = a
        args.append(nc.dram_tensor(f"in_{name}_dram", a.shape, _mybir.dt.from_np(a.dtype), kind="ExternalInput").ap())
    shape = _np.asarray(inputs['x']).shape
    args.append(nc.dram_tensor("out_0_dram", shape, _mybir.dt.float32, kind="ExternalOutput").ap())
    build(nc, *args)
    r = _run(nc, [arrays], core_ids=[0])
    return r.results[0]["out_0_dram"]
```

```python
from contextlib import ExitStack

import concourse.bass as bass
from concourse import mybir

ALU = mybir.AluOpType
ACT = mybir.ActivationFunctionType
F32 = mybir.dt.float32
I32 = mybir.dt.int32
BF16 = mybir.dt.bfloat16
F16 = mybir.dt.float16
AX_X = mybir.AxisListType.X
ds = bass.ds

P = 128
D = 64
T = 8
GE = P * T
W = 40
RING = 3
NP = 125
BLK = 5
CN = NP * BLK
BC = BLK * D
WT = 7
BATCH = 22
DRING = BATCH // 2
PAIRS = BATCH // 2
SUM_AFTER = (3, 7, 10)
PARTS = 3
FAR = -20000.0


def steps(eng, count, unroll, body, between=None, beside=None, times=0):
    assert count % unroll == 0
    for slot in range(unroll):
        body(slot, slot)
    if between:
        between()
    if times:
        with eng.Fori(1, 1 + times) as turn:
            beside(turn)
            for slot in range(unroll):
                body(turn * unroll + slot, slot)
    with eng.Fori(1 + times, count // unroll) as turn:
        for slot in range(unroll):
            body(turn * unroll + slot, slot)


def piped(eng, count, unroll, stages, between=None, alone=None):
    assert count % unroll == 0
    longest = max(lag for lag, _ in stages)
    alone = alone or -(-max(longest, 1) // unroll) * unroll

    def step(c, s):
        for lag, body in stages:
            if not isinstance(c, int) or 0 <= c - lag < count:
                body(c - lag, (s - lag) % unroll)

    for c in range(alone):
        step(c, c % unroll)
    if between:
        between()
    with eng.Fori(alone // unroll, count // unroll) as turn:
        for s in range(unroll):
            step(turn * unroll + s, s)
    for c in range(count, count + longest):
        step(c, c % unroll)


def wait_step(eng, sem, g, each=1):
    if not isinstance(g, int) or g >= 0:
        eng.wait_ge(sem, (g + 1) * each)


def build(nc, x, src, dst, edge_attr, edge_weight, w1, b1, w2, b2, u1, c1, u2, c2, out):
    N = x.shape[0]
    E = src.shape[0]
    NB = N // NP
    CHUNKS = NB // BLK
    FULL = E // GE
    GROUPS = FULL + 1
    OVERLAP = FULL * GE - (E - GE)
    BATCHES = 35
    TILES = BATCHES * BATCH
    HALF = (GROUPS - TILES // T, TILES // T)
    REAL = HALF[1] * T
    NHI = -(-N // P)
    NLAST = N - (NHI - 1) * P
    PARAMETERS = 9
    WINDOWS = -(-N // W)
    assert HALF[0] % RING == 1 and HALF[0] > RING * BATCHES and BATCHES % 2 == 1 and SUM_AFTER[-1] == PAIRS - 1
    assert N == NB * NP and NB == CHUNKS * BLK and CHUNKS % 2 == 0 and FULL % RING == 0

    table1 = nc.dram_tensor("table1", (N, D), F32, kind="Internal").ap()
    table2 = nc.dram_tensor("table2", (N, D), F32, kind="Internal").ap()

    with ExitStack() as ctx:
        def sb(name, shape, dt=F32):
            return ctx.enter_context(nc.sbuf_tensor(name, shape, dt))

        def psum(name, shape):
            return ctx.enter_context(nc.psum_tensor(name, shape, F32))

        def sem(name):
            return ctx.enter_context(nc.semaphore(name))

        x_all = sb("x_all", [NP, NB * D])
        mid = sb("mid", [P, NB * D])
        cent = mid[0:NP, :]
        h2 = mid[:, 0:(NHI - 1) * D].rearrange("p (h f) -> p h f", f=D)
        h2_last = sb("h2_last", [P, D])
        row_sum = sb("row_sum", [NP, NB])
        mean = sb("mean", [NP, NB])
        var = sb("var", [NP, NB])
        std = sb("std", [NP, NB])
        rstd = sb("rstd", [NP, NB])
        stages = sb("stages", [P, max(2 * BC, DRING * P // 2)])
        h_stage = stages[0:NP, 0:2 * BC].rearrange("p (s f) -> p s f", s=2)
        nodes = sb("nodes", [P, 2 * N + W])
        node_cols = nodes[:, 0:N]
        hT = node_cols[0:D + 1, :]
        acc1 = nodes[0:D + 1, N:]
        late = sb("late", [P, N + W])
        acc2 = late[0:D, :]
        t_stage = sb("t_stage", [D + 1, 2, CN])
        early = late[:, 0:6 * GE].rearrange("g (k h e) -> g k h e", k=3, h=2)
        wgt_g = early[:, 0]
        dst_i = early[:, 1].bitcast(I32)
        src_i = early[:, 2].bitcast(I32)
        key_g = sb("key_g", [P, GE])
        hi = sb("hi", [P, 2])
        lo = sb("lo", [P, 2])
        base = sb("base", [P, 2])
        bad = sb("bad", [P, 3])
        above = sb("above", [P, 2])
        bad_all = sb("bad_all", [P, 1])
        fast_f = sb("fast_f", [P, 1])
        fast_i = sb("fast_i", [P, 1], I32)
        base_row = sb("base_row", [1, GROUPS], I32)
        rel = sb("rel", [P, GROUPS, T])
        idx = sb("idx", [P, GROUPS + RING, T], I32)
        wgt = sb("wgt", [P, GROUPS, T])
        idx_ring = sb("idx_ring", [P, RING, T], I32)
        rings = sb("rings", [P, 3 * RING * T * D + RING * T * (D + 1) + 2 * GE])
        ea_ring = rings[:, 0:RING * T * D].rearrange("p (s f) -> p s f", s=RING)
        eaT = rings[:, RING * T * D:2 * RING * T * D].rearrange("p (s a e) -> p s a e", s=RING, e=P)
        pre = rings[:, 2 * RING * T * D:3 * RING * T * D].rearrange("p (s t f) -> p s t f", s=RING, f=D)
        hid_end = 3 * RING * T * D + RING * T * (D + 1)
        hid = rings[:, 3 * RING * T * D:hid_end].rearrange("p (s t f) -> p s t f", s=RING, f=D + 1)
        rows = sb("rows", [P, RING, T, D])
        sq = rows[0:NP, 0:2, 0:BLK, :].rearrange("p s b f -> p s (b f)")
        row_all = rings[0:NP, 0:NB * D]
        adjacency = [nodes[:, 0:NHI * BATCH * WT].rearrange("p (h c) -> p h c", h=NHI),
                     rings[:, 0:NHI * BATCH * WT].rearrange("p (h c) -> p h c", h=NHI)]
        src_f = [key_g[0:HALF[0], :], rings[0:HALF[1], NB * D:NB * D + GE]]
        assert NB * D + GE <= 3 * RING * T * D
        d_key = rings[0:HALF[1], hid_end:hid_end + GE]
        d_hi = rings[0:HALF[1], hid_end + GE:hid_end + 2 * GE].bitcast(I32)
        assert hid_end + 2 * GE >= NHI * BATCH * WT
        t_base = sb("t_base", [HALF[1], T])
        t_hi = sb("t_hi", [HALF[1], 1])
        t_lo = sb("t_lo", [HALF[1], 1])
        t_above = sb("t_above", [HALF[1], 1])
        tile_row = sb("tile_row", [1, TILES], I32)
        tile_tab = sb("tile_tab", [P, 2 + PARTS, TILES])

        def by_turn(ap):
            return ap[:, 0:REAL].rearrange("p (g t) -> p t g", t=T)

        tile_key = tile_tab[:, 0, :]
        tile_lo = tile_tab[:, 1, :]
        tile_w = tile_tab[:, 2:, 0:REAL]
        key_bf = key_g[:, :].bitcast(BF16)
        tile_wb = key_bf[:, 0:REAL]
        tile_now = sb("tile_now", [P, 2, 2 + PARTS, BATCH])
        hot_key = sb("hot_key", [P, DRING, NHI * WT], BF16)

        def hot_ring(flat):
            return flat.bitcast(BF16)[:, 0:DRING * P].rearrange("p (s e) -> p s e", s=DRING)

        hot_eq = hot_ring(rel[:, HALF[0]:, :].rearrange("p g t -> p (g t)"))
        hot_w = [hot_ring(key_g[:, :]), hot_ring(stages[:, :]),
                 hot_ring(wgt[:, HALF[0]:, :].rearrange("p g t -> p (g t)"))]
        iota_key = sb("iota_key", [P, NHI * WT], F16)
        hot = sb("hot", [P, RING, T, W])
        key_now = sb("key_now", [P, RING, T])
        ident = sb("ident", [P, P])
        ones = sb("ones", [P, P])
        iota = sb("iota", [P, W])
        eps = sb("eps", [P, 1])
        w1a = sb("w1a", [D + 1, D])
        w1b2 = sb("w1b2", [P, P])
        w2b = sb("w2b", [D + 1, D])
        w2bT = sb("w2bT", [D, D + 1])
        w2u = sb("w2u", [D + 1, D])
        u1a = sb("u1a", [D + 1, D])
        u1b = sb("u1b", [D, D])
        u2_s = sb("u2_s", [D + 1, D])

        pair = [psum(f"pair{i}", [P, 2, 512]) for i in range(4)]

        def wide(slot):
            return pair[slot][0:D, :, :].rearrange("f b n -> f (b n)")[:, 0:BLK * P].rearrange(
                "f (b n) -> f b n", n=P)

        def tall(slot):
            return pair[2][0:NP, slot, 0:BC]

        x_begun = sem("x_begun")
        x_loaded = sem("x_loaded")
        w1_loaded = sem("w1_loaded")
        src_loaded = sem("src_loaded")
        dst_loaded = sem("dst_loaded")
        wgt_loaded = sem("wgt_loaded")
        par_loaded = sem("par_loaded")
        consts_set = sem("consts_set")
        t_base_made = sem("t_base_made")
        t_rel_made = sem("t_rel_made")
        t_range_made = sem("t_range_made")
        t_above_made = sem("t_above_made")
        t_hi_made = sem("t_hi_made")
        t_lo_made = sem("t_lo_made")
        w_split = sem("w_split")
        h2_loaded = sem("h2_loaded")
        columns_staged = sem("columns_staged")
        pair_hot = sem("pair_hot")
        pair_made = sem("pair_made")
        pair_kept = sem("pair_kept")
        tile_added = sem("tile_added")
        batch_added = sem("batch_added")
        pair_scaled = sem("pair_scaled")
        applied = sem("applied")
        pool_step = sem("pool_step")
        pe_held = sem("pe_held")
        pool_held = sem("pool_held")
        ones_set = sem("ones_set")
        key_made = sem("key_made")
        key_turned = sem("key_turned")
        key_kept = sem("key_kept")
        range_made = sem("range_made")
        bad_made = sem("bad_made")
        bad_summed = sem("bad_summed")
        fast_made = sem("fast_made")
        base_turned = sem("base_turned")
        base_made = sem("base_made")
        w2_turned = sem("w2_turned")
        w2_kept = sem("w2_kept")
        w2u_made = sem("w2u_made")
        w2u_kept = sem("w2u_kept")
        ln_sum = sem("ln_sum")
        ln_mean = sem("ln_mean")
        ln_cent = sem("ln_cent")
        ln_sq = sem("ln_sq")
        ln_var = sem("ln_var")
        ln_std = sem("ln_std")
        ln_rstd = sem("ln_rstd")
        h_staged = sem("h_staged")
        h_turned = sem("h_turned")
        hT_staged = sem("hT_staged")
        t1_made = sem("t1_made")
        t1_staged = sem("t1_staged")
        t1_stored = [sem(f"t1_stored{s}") for s in range(2)]
        idx_ready = sem("idx_ready")
        gathered = [sem(f"gathered{s}") for s in range(RING)]
        ea_loaded = [sem(f"ea_loaded{s}") for s in range(RING)]
        ea_turned = sem("ea_turned")
        eaT_kept = sem("eaT_kept")
        q_made = sem("q_made")
        pre_made = sem("pre_made")
        hid_made = sem("hid_made")
        hot_made = sem("hot_made")
        hot_weighed = sem("hot_weighed")
        acc_added = sem("acc_added")
        turn_made = sem("turn_made")
        group_done = sem("group_done")
        above_made = sem("above_made")
        bad_counted = sem("bad_counted")
        last_made = sem("last_made")
        key_moved = sem("key_moved")
        whot_made = sem("whot_made")
        whot_weighed = sem("whot_weighed")
        wseg_made = sem("wseg_made")
        wacc_added = sem("wacc_added")
        part_made = sem("part_made")
        part_kept = sem("part_kept")
        g_made = sem("g_made")
        g_summed = sem("g_summed")
        g_staged = sem("g_staged")
        up_made = sem("up_made")
        x1_made = sem("x1_made")
        h2_staged = sem("h2_staged")
        t2_stored = [sem(f"t2_stored{s}") for s in range(2)]
        a_staged = sem("a_staged")
        a_turned = sem("a_turned")
        out_staged = sem("out_staged")
        out_stored = [sem(f"out_stored{s}") for s in range(2)]

        def build_banks(r):
            return pair[r % 2][:, :, 0:NHI * WT]

        def blocks(dram, c):
            return dram[ds(c * CN, CN), :].rearrange("(b p) f -> p b f", p=NP)

        def chunked(t, c):
            return t[:, ds(c * BC, BC)]

        def by_block(ap):
            return ap.rearrange("p (b f) -> p b f", f=D)

        def of_chunk(ap, c):
            return ap[:, ds(c * BLK, BLK)]

        def spread(ap, n):
            return ap.rearrange("p (b o) -> p b o", o=1).to_broadcast([ap.shape[0], ap.shape[1], n])

        def edge_row(place):
            return E - GE if isinstance(place, int) and place == 0 else (place - 1) * GE

        def gathered_wait(eng, g, slot, before):
            turns = -(-(before - slot) // RING) if before else 0
            if isinstance(g, int):
                eng.wait_ge(gathered[slot], (g // RING + 1 + turns) * 16 * T)
            else:
                eng.wait_ge(gathered[slot], ((g - slot) // RING + 1 + turns) * 16 * T)

        def dense_turns(eng, body):
            steps(eng, BATCHES - 1, 2, body)
            body(BATCHES - 1, 0)

        def rest_of_half(eng, body):
            for g in range(RING * BATCHES, HALF[0]):
                body(g, g % RING)

        block = ctx.enter_context(nc.Block())

        @block.sync
        def _(sp):
            for c in range(0, CHUNKS, 2):
                sp.dma_start(by_block(x_all[:, c * BC:(c + 2) * BC]),
                             x[c * CN:(c + 2) * CN, :].rearrange("(b p) f -> p b f", p=NP)
                             ).then_inc(x_loaded if c else x_begun, 16)

            def load_groups(tile, dram, loaded):
                sp.dma_start(tile[0:1, 0, :], dram[E - GE:E].rearrange("(o e) -> o e", o=1)).then_inc(loaded, 16)
                split = (HALF[0] - 1) * GE
                sp.dma_start(tile[1:HALF[0], 0, :],
                             dram[0:split].rearrange("(g e) -> g e", e=GE)).then_inc(loaded, 16)
                sp.dma_start(tile[0:HALF[1], 1, :],
                             dram[split:FULL * GE].rearrange("(g e) -> g e", e=GE)).then_inc(loaded, 16)

            load_groups(src_i, src, src_loaded)
            load_groups(dst_i, dst, dst_loaded)
            load_groups(wgt_g, edge_weight, wgt_loaded)

            def load_ea(g, slot):
                wait_step(sp, ea_turned, g - RING)
                rows_of = edge_attr[ds(edge_row(g), GE), :].rearrange("(p t) f -> p (t f)", t=T)
                sp.dma_start(ea_ring[:, slot, :], rows_of).then_inc(ea_loaded[slot], 16)

            def store_t1(c, slot):
                wait_step(sp, t1_staged, c)
                sp.dma_start(blocks(table1, c), by_block(chunked(row_all, c))).then_inc(t1_stored[slot], 16)

            steps(sp, CHUNKS, 2, store_t1)
            for s in range(2):
                sp.wait_ge(t1_stored[s], 16 * CHUNKS // 2)
            steps(sp, FULL, RING, load_ea)
            load_ea(FULL, 0)

            def store_t2(c, slot):
                wait_step(sp, h2_staged, c)
                sp.dma_start(blocks(table2, c), by_block(chunked(row_all, c))).then_inc(t2_stored[slot], 16)

            steps(sp, CHUNKS, 2, store_t2)
            for s in range(2):
                sp.wait_ge(t2_stored[s], 16 * CHUNKS // 2)
            sp.dma_start(h2, table2[0:(NHI - 1) * P, :].rearrange("(h p) f -> p h f", p=P)).then_inc(h2_loaded, 16)
            sp.dma_start(h2_last[0:NLAST, :], table2[(NHI - 1) * P:N, :]).then_inc(h2_loaded, 16)

            def store_out(c, slot):
                wait_step(sp, out_staged, c)
                sp.dma_start(blocks(out, c), by_block(chunked(x_all, c))).then_inc(out_stored[slot], 16)

            steps(sp, CHUNKS, 2, store_out)
            for s in range(2):
                sp.wait_ge(t1_stored[s], 16 * CHUNKS // 2)
                sp.wait_ge(t2_stored[s], 16 * CHUNKS // 2)
                sp.wait_ge(out_stored[s], 16 * CHUNKS // 2)
            sp.wait_ge(h2_loaded, 32)

        @block.gpsimd
        def _(pool):
            pool.memset(eps[:, :], 1e-5).then_inc(consts_set, 1)
            pool.memset(ones[:, :], 1.0).then_inc(consts_set, 1)
            pool.memset(ident[:, :], 0.0).then_inc(pool_step, 1)
            pool.memset(w1b2[:, :], 0.0).then_inc(pool_step, 1)
            pool.wait_ge(pool_step, 2)
            pool.affine_select(out=ident[:, :], in_=ident[:, :], compare_op=ALU.not_equal, fill=1.0, base=0,
                               pattern=[[-1, P]], channel_multiplier=1).then_inc(consts_set, 1)
            pool.iota(iota[:, :], [[1, W]], base=0, channel_multiplier=0,
                      allow_small_or_imprecise_dtypes=True).then_inc(consts_set, 1)
            pool.memset(bad[:, :], 0.0).then_inc(consts_set, 1)
            pool.memset(t_stage[:, :, :], 1.0).then_inc(consts_set, 1)
            pool.dma_start(w1a[0:D, :], w1[0:D, :]).then_inc(w1_loaded, 16)
            pool.dma_start(w1a[D:D + 1, :], b1.rearrange("(o f) -> o f", o=1)).then_inc(w1_loaded, 16)
            for to, of in ((w1b2[0:D, 0:D], w1[D:2 * D, :]),
                           (w1b2[D:P, D:P], w1[D:2 * D, :]), (w2b[0:D, :], w2),
                           (w2b[D:D + 1, :], b2.rearrange("(o f) -> o f", o=1)),
                           (u1a[0:D, :], u1[0:D, :]), (u1b[:, :], u1[D:2 * D, :]), (u2_s[0:D, :], u2),
                           (u1a[D:D + 1, :], c1.rearrange("(o f) -> o f", o=1)),
                           (u2_s[D:D + 1, :], c2.rearrange("(o f) -> o f", o=1))):
                pool.dma_start(to, of).then_inc(par_loaded, 16)
            pool.iota(iota_key[:, :], [[1, NHI * WT]], base=0, channel_multiplier=0,
                      allow_small_or_imprecise_dtypes=True).then_inc(consts_set, 1)
            pool.memset(h2_last[:, :], 0.0).then_inc(consts_set, 1)
            pool.memset(hid[:, :, :, D:D + 1], 1.0).then_inc(consts_set, 1)
            pool.memset(idx[:, GROUPS:, :], 0).then_inc(consts_set, 1)
            pool.memset(tile_tab[:, :, REAL:], FAR).then_inc(consts_set, 1)
            pool.memset(tile_row[:, REAL:], 0).then_inc(consts_set, 1)
            pool.wait_ge(src_loaded, 48)
            for k in range(2):
                pool.tensor_copy(src_f[k], src_i[0:HALF[k], k, :]).then_inc(key_made, 1)
            pool.memset(acc1[:, :], 0.0).then_inc(consts_set, 1)

            def gather(table, g, slot, used, before, refills):
                wait_step(pool, idx_ready, g + refills)
                wait_step(pool, used, g - RING + before)
                pool.sem_inc(pool_held, 1)
                for t in range(T):
                    pool.indirect_dma_start(
                        out=rows[:, slot, t, :], out_offset=None, in_=table,
                        in_offset=bass.IndirectOffsetOnAxis(ap=idx_ring[:, slot, t:t + 1], axis=0),
                    ).then_inc(gathered[slot], 16)

            pool.wait_ge(key_made, 2)
            pool.wait_ge(consts_set, 13)
            pool.memset(hT[D:D + 1, :], 1.0).then_inc(ones_set, 1)
            for s in range(2):
                pool.wait_ge(t1_stored[s], 16 * CHUNKS // 2)
            steps(pool, FULL, RING, lambda g, slot: gather(table1, g, slot, pre_made, 0, 0))
            gather(table1, FULL, 0, pre_made, 0, 0)
            pool.wait_ge(pre_made, GROUPS)
            for s in range(2):
                pool.wait_ge(t2_stored[s], 16 * CHUNKS // 2)
            def gather2(g, slot):
                gather(table2, g, slot, group_done, GROUPS, GROUPS + RING)

            pool.wait_ge(fast_made, 2)
            fast = pool.value_load(fast_i[0:1, 0:1], min_val=0, max_val=1)
            with pool.If(fast > 0):
                steps(pool, HALF[0] - 1, RING, gather2)
                gather2(HALF[0] - 1, 0)
            with pool.Else():
                steps(pool, FULL, RING, gather2)
                gather2(FULL, 0)

        @block.scalar
        def _(act):
            def square(n):
                def body(c, slot):
                    wait_step(act, ln_cent, c + (n - 1) * CHUNKS)
                    act.activation(sq[:, slot, :], chunked(cent, c), ACT.Square).then_inc(ln_sq, 1)
                return body

            def root(n):
                def body(c, slot):
                    wait_step(act, ln_var, c + (n - 1) * CHUNKS)
                    act.activation(of_chunk(std, c), of_chunk(var, c), ACT.Sqrt, bias=eps[0:NP, :],
                                   scale=1.0 / D).then_inc(ln_std, 1)
                return body

            def refill_idx(g, slot):
                act.copy(idx_ring[:, slot, :], idx[:, ds(g, 1), :].rearrange("p o t -> p (o t)")
                         if not isinstance(g, int) else idx[:, g, :]).then_inc(idx_ready, 1)

            act.wait_ge(consts_set, 1)
            act.activation(fast_f[0:NP, :], eps[0:NP, :], ACT.Sqrt)

            def stage_hT(c, slot):
                wait_step(act, h_turned, c)
                wait_step(act, t1_made, c - 2)
                act.copy(t_stage[0:D, slot, :].rearrange("f (b n) -> f b n", n=NP), wide(slot)[:, :, 0:NP])
                act.copy(hT[0:D, ds(c * CN, CN)].rearrange("f (b n) -> f b n", n=NP),
                         wide(slot)[:, :, 0:NP]).then_inc(hT_staged, 1)

            def stage_t1(c, slot):
                wait_step(act, t1_made, c)
                act.copy(chunked(row_all, c), tall(slot)).then_inc(t1_staged, 1)

            def keep(k, to):
                h = k % 2
                g0, n = h * HALF[0], HALF[h]
                for q in range(2):
                    act.wait_ge(key_turned, 2 * k + q + 1)
                    act.copy(to[:, g0:g0 + n, 4 * q:4 * q + 4].rearrange("p g t -> p t g"),
                             pair[3][:, q, :].rearrange("p (t g) -> p t g", g=P)[:, :, 0:n]).then_inc(key_kept, 1)

            def keep_sources():
                for k in range(2):
                    keep(k, idx)

            piped(act, CHUNKS, 2, ((1, root(1)), (0, square(1)), (2, stage_hT), (3, stage_t1)), keep_sources, 8)

            act.wait_ge(consts_set, 13)
            act.wait_ge(key_kept, 4)
            for s in range(RING):
                refill_idx(s, s)
            act.wait_ge(base_turned, 2)
            for h in range(2):
                last = act.copy(base_row[:, h * HALF[0]:h * HALF[0] + HALF[h]],
                                pair[3][0:1, 1, h * P:h * P + HALF[h]])
            last.then_inc(base_made, 1)
            for k in range(2, 4):
                keep(k, rel)

            def pass1(g, slot):
                wait_step(act, ea_turned, g)
                wait_step(act, q_made, g - RING)
                act.copy(eaT[:, slot, :, :].rearrange("p a e -> p (a e)"), pair[slot][:, 0, :]).then_inc(eaT_kept, 1)
                wait_step(act, pre_made, g)
                wait_step(act, group_done, g - RING)
                act.activation(hid[:, slot, :, 0:D], pre[:, slot, :, :], ACT.Relu).then_inc(hid_made, 1)
                refill_idx(g + RING, slot)

            def clear_sums():
                act.wait_ge(key_kept, 20)
                act.activation(acc2, ones[0:D, 0:1].to_broadcast([D, N + W]), ACT.Copy,
                               scale=0.0).then_inc(batch_added, 1)
                act.sem_inc(part_kept, 1)

            def keep_part(turn):
                act.wait_ge(part_made, turn)
                act.copy(hT[0:D, ds((turn - 1) * NP, NP)], pair[3][0:D, 1, 0:NP]).then_inc(part_kept, 1)

            steps(act, FULL, RING, pass1, clear_sums, keep_part, NB)
            pass1(FULL, 0)

            def stage_g(c, slot):
                wait_step(act, g_summed, c)
                act.activation(t_stage[0:D, slot, :], t_stage[0:D, slot, :], ACT.Relu).then_inc(g_staged, 1)

            piped(act, CHUNKS, 2, ((0, stage_g), (2, root(2)), (1, square(2))))

            for s in range(RING):
                refill_idx(s, s)

            def pass2(g, slot):
                wait_step(act, group_done, g + GROUPS)
                refill_idx(g + RING, slot)

            def scale_pair(n, b, r):
                act.wait_ge(pair_hot, r + 1)
                for i in (2 * n, 2 * n + 1):
                    for k in (1, 2):
                        last = act.activation(hot_w[k][:, i % DRING, :], hot_eq[:, i % DRING, :], ACT.Copy,
                                              scale=tile_now[:, b, 2 + k, i:i + 1])
                last.then_inc(pair_scaled, 1)

            def dense_turn(j, b):
                for n in range(PAIRS):
                    r = j * PAIRS + n
                    if not isinstance(j, int) or r + 1 < BATCHES * PAIRS:
                        scale_pair((n + 1) % PAIRS, (b + (n + 1) // PAIRS) % 2, r + 1)
                    if n == 0 and (not isinstance(j, int) or j >= 2):
                        act.wait_ge(applied, j - 1)
                    act.wait_ge(pair_made, r + 1)
                    act.copy(adjacency[b][:, :, n * 2 * WT:(n + 1) * 2 * WT].rearrange("p h (t w) -> p t h w", t=2),
                             build_banks(b + n).rearrange("p t (h w) -> p t h w", w=WT)).then_inc(pair_kept, 1)
                    if n % 4 == 1 and (n > 1 or not isinstance(j, int) or j):
                        u = n // 4
                        pass2(j * RING + u - 1, (u - 1) % RING)

            act.wait_ge(fast_made, 2)
            fast = act.value_load(fast_i[0:1, 0:1], min_val=0, max_val=1)
            with act.If(fast > 0):
                for s in range(2):
                    act.wait_ge(t1_stored[s], 16 * CHUNKS // 2)
                    act.wait_ge(t2_stored[s], 16 * CHUNKS // 2)
                scale_pair(0, 0, 0)
                dense_turns(act, dense_turn)
                pass2(RING * BATCHES - 1, RING - 1)
                rest_of_half(act, pass2)
            with act.Else():
                steps(act, FULL, RING, pass2)
                pass2(FULL, 0)
            act.wait_ge(turn_made, 2)

            def stage_a(c, slot):
                wait_step(act, a_turned, c - 2)
                act.copy(t_stage[0:D, slot, :], acc2[:, ds(c * CN, CN)]).then_inc(a_staged, 1)

            steps(act, CHUNKS, 2, stage_a)

        @block.tensor
        def _(pe):
            def hold():
                pe.sem_inc(pe_held, 1)

            pe.wait_ge(consts_set, 6)
            def turn(k):
                h = k % 2 if k < 6 else 1
                n = HALF[h]
                if k in (4, 5):
                    pe.wait_ge(wgt_loaded, 48)
                if k not in (4, 5, 8, 9):
                    pe.wait_ge(key_made, k + 1 if k < 4 else k - 1)
                for q in range(2):
                    if 2 * k + q >= 2:
                        pe.wait_ge(key_kept, 2 * k + q - 1)
                    for t in range(4 * q, 4 * q + 4):
                        if k < 6:
                            of = src_f[k] if k < 2 else key_g[0:n, :] if k < 4 else wgt_g[0:n, h, :]
                            of = of.rearrange("g (p t) -> g t p", t=T)[:, t, :]
                        elif k < 9:
                            of = (d_key, key_g[0:n, :], wgt_g[0:n, 1, :])[k - 6][:, t * P:(t + 1) * P]
                        else:
                            of = t_base[:, t:t + 1]
                        last = pe.transpose(pair[3][0:of.shape[1], q, (t % 4) * P:(t % 4) * P + n], of, ident[0:n, 0:n])
                    last.then_inc(key_turned, 1)

            def turn_sources():
                for k in range(2):
                    turn(k)

            def turn_h(c, slot):
                wait_step(pe, h_staged, c)
                wait_step(pe, hT_staged, c - 2)
                hold()
                for b in range(BLK):
                    last = pe.transpose(wide(slot)[:, b, 0:NP], h_stage[:, slot, b * D:(b + 1) * D],
                                        ident[0:NP, 0:NP])
                last.then_inc(h_turned, 1)

            def make_t1(c, slot):
                wait_step(pe, hT_staged, c)
                wait_step(pe, t1_staged, c - 2)
                if isinstance(c, int) and c == 0:
                    pe.wait_ge(w1_loaded, 32)
                for b in range(BLK):
                    last = pe.matmul(tall(slot)[:, b * D:(b + 1) * D], t_stage[:, slot, b * NP:(b + 1) * NP],
                                     w1a[:, :], start=True, stop=True)
                last.then_inc(t1_made, 1)

            piped(pe, CHUNKS, 2, ((0, turn_h), (1, make_t1)), turn_sources, 6)

            pe.wait_ge(key_kept, 4)
            pe.wait_ge(par_loaded, 16 * PARAMETERS)
            pe.transpose(pair[3][0:D, 0, 0:D + 1], w2b[:, :], ident[0:D + 1, 0:D + 1]).then_inc(w2_turned, 1)
            pe.wait_ge(w2_kept, 1)
            pe.matmul(pair[3][0:D + 1, 1, 0:D], w2bT[:, :], u1b[:, :], start=True, stop=True).then_inc(w2u_made, 1)
            pe.wait_ge(w2u_kept, 1)

            pe.wait_ge(key_kept, 4)
            pe.wait_ge(bad_made, 3)
            pe.matmul(pair[3][:, 0, 0:3], ones[:, :], bad[:, :], start=True, stop=True).then_inc(bad_summed, 1)
            for h in range(2):
                pe.wait_ge(range_made, 3 * 2 + 1 + h)
                pe.transpose(pair[3][0:1, 1, h * P:h * P + HALF[h]], base[0:HALF[h], h:h + 1],
                             ident[0:HALF[h], 0:HALF[h]]).then_inc(base_turned, 1)
            pe.wait_ge(base_made, 1)
            for k in range(2, 4):
                turn(k)
            def make_part(turn):
                pe.wait_ge(part_kept, turn)
                hold()
                pe.matmul(pair[3][0:D, 1, 0:NP], u1a[:, :], hT[:, ds((turn - 1) * NP, NP)],
                          start=True, stop=True).then_inc(part_made, 1)

            pe.wait_ge(ones_set, 1)

            def turn_rest():
                for k in range(4, 10):
                    turn(k)
                pe.wait_ge(key_kept, 20)

            def turn_rest_fast():
                pe.wait_ge(acc_added, RING)
                turn_rest()

            pe.wait_ge(key_kept, 8)
            pe.wait_ge(consts_set, 13)
            pe.wait_ge(fast_made, 2)
            fast = pe.value_load(fast_i[0:1, 0:1], min_val=0, max_val=1)

            def products(g, slot):
                pe.wait_ge(ea_loaded[slot], g // RING * 16 + 16) if isinstance(g, int) else \
                    pe.wait_ge(ea_loaded[slot], (g - slot) // RING * 16 + 16)
                wait_step(pe, eaT_kept, g - RING)
                for a in range(T // 2):
                    last = pe.transpose(pair[slot][:, 0, a * P:(a + 1) * P],
                                        ea_ring[:, slot, a * P:(a + 1) * P], ident[:, :])
                last.then_inc(ea_turned, 1)
                wait_step(pe, eaT_kept, g)
                wait_step(pe, pre_made, g - RING)
                for a in range(T // 2):
                    last = pe.matmul(pair[slot][:, 1, a * P:(a + 1) * P], eaT[:, slot, a, :], w1b2[:, :],
                                     start=True, stop=True)
                last.then_inc(q_made, 1)

            def segment(lhs, slot, bank, m):
                for t in range(T):
                    last = pe.matmul(pair[3][0:m, bank, 0:W], lhs[:, slot, t, 0:m], hot[:, slot, t, :],
                                     start=(t == 0), stop=(t == T - 1))
                return last

            def fast1(g, slot):
                products(g, slot)
                wait_step(pe, hot_made, g)
                wait_step(pe, hid_made, g)
                wait_step(pe, acc_added, g - 1)
                segment(hid, slot, 0, D + 1).then_inc(group_done, 1)

            def segment2(g, slot, bank):
                wait_step(pe, hot_weighed, g)
                gathered_wait(pe, g, slot, GROUPS)
                segment(rows, slot, bank, D).then_inc(group_done, 1)

            def apply(b, low, high):
                for hi in range(low, high):
                    of = h2_last[:, :] if hi == NHI - 1 else h2[:, hi, :]
                    last = pe.matmul(pair[2][0:D, b % 2, 0:BATCH * WT], of, adjacency[b % 2][:, hi, :],
                                     start=(hi == 0), stop=(hi == NHI - 1))
                return last

            def dense_turn(j, b):
                for n in range(PAIRS):
                    r = j * PAIRS + n
                    pe.wait_ge(pair_scaled, r + 1)
                    wait_step(pe, pair_kept, r - 2)
                    for i in (2 * n, 2 * n + 1):
                        for k in range(PARTS):
                            last = pe.matmul(build_banks(b + n)[:, i % 2, :], hot_w[k][:, i % DRING, :],
                                             hot_key[:, i % DRING, :], start=(k == 0), stop=(k == PARTS - 1))
                    last.then_inc(pair_made, 1)
                    if not (isinstance(j, int) and j == 0):
                        if n == 0:
                            pe.wait_ge(pair_kept, j * PAIRS)
                            if isinstance(j, int) and j == 1:
                                pe.wait_ge(h2_loaded, 32)
                            else:
                                pe.wait_ge(batch_added, j - 1)
                        last = apply(1 - b, n * NHI // PAIRS, (n + 1) * NHI // PAIRS)
                        if n == PAIRS - 1:
                            last.then_inc(applied, 1)
                    if n in SUM_AFTER:
                        u = SUM_AFTER.index(n)
                        wait_step(pe, acc_added, j * RING + u - 2 + GROUPS)
                        segment2(j * RING + u, u, (b * RING + u) % 2)

            def slow1(g, slot):
                products(g, slot)
                wait_step(pe, hid_made, g)
                windows(lambda: segment(hid, slot, 0, D + 1), whot_made, g, g)

            def slow2(g, slot):
                gathered_wait(pe, g, slot, GROUPS)
                windows(lambda: segment(rows, slot, 0, D), whot_weighed, g, g + GROUPS)

            def windows(product, made, g_made, g_done):
                hold()
                with pe.Fori(0, WINDOWS) as k:
                    pe.wait_ge(made, g_made * WINDOWS + k + 1)
                    product().then_inc(wseg_made, 1)
                    pe.wait_ge(wacc_added, g_done * WINDOWS + k + 1)
                pe.nop().then_inc(group_done, 1)

            with pe.If(fast > 0):
                steps(pe, FULL, RING, fast1, turn_rest_fast, make_part, NB)
                fast1(FULL, 0)
            with pe.Else():
                steps(pe, FULL, RING, slow1, turn_rest, make_part, NB)
                slow1(FULL, 0)

            pe.wait_ge(turn_made, 1)

            def make_g(c, slot):
                wait_step(pe, g_summed, c - 2)
                for b0, nb in ((0, 4), (4, 1)):
                    last = pe.matmul(wide(slot)[:, b0:b0 + nb, 0:NP], w2u[:, :],
                                     acc1[:, ds(c * CN + b0 * NP, nb * NP)].rearrange("f (b n) -> f b n", n=NP),
                                     start=True, stop=True)
                last.then_inc(g_made, 1)

            def make_up(c, slot):
                wait_step(pe, g_staged, c)
                wait_step(pe, x1_made, c - 2)
                for b in range(BLK):
                    last = pe.matmul(tall(slot)[:, b * D:(b + 1) * D], t_stage[:, slot, b * NP:(b + 1) * NP],
                                     u2_s[:, :], start=True, stop=True)
                last.then_inc(up_made, 1)

            piped(pe, CHUNKS, 2, ((0, make_g), (1, make_up)))

            pe.wait_ge(x1_made, CHUNKS)
            with pe.If(fast > 0):
                dense_turns(pe, dense_turn)
                pe.wait_ge(pair_kept, BATCHES * PAIRS)
                pe.wait_ge(batch_added, BATCHES - 1)
                apply(BATCHES - 1, 0, NHI).then_inc(applied, 1)

                def rest(g, slot):
                    pe.wait_ge(acc_added, g + GROUPS)
                    segment2(g, slot, 0)

                rest_of_half(pe, rest)
            with pe.Else():
                steps(pe, FULL, RING, slow2)
                slow2(FULL, 0)

            def chunk3(c, slot):
                wait_step(pe, a_staged, c)
                wait_step(pe, out_staged, c - 2)
                hold()
                for b in range(BLK):
                    last = pe.transpose(tall(slot)[:, b * D:(b + 1) * D], t_stage[0:D, slot, b * NP:(b + 1) * NP],
                                        ident[0:D, 0:D])
                last.then_inc(a_turned, 1)

            steps(pe, CHUNKS, 2, chunk3)

        @block.vector
        def _(dve):
            def centre(n):
                def body(c, slot):
                    k = c + (n - 1) * CHUNKS
                    dve.tensor_reduce(of_chunk(row_sum, c), by_block(chunked(x_all, c)), AX_X,
                                      ALU.add).then_inc(ln_sum, 1)
                    wait_step(dve, ln_sum, k)
                    dve.tensor_scalar(of_chunk(mean, c), of_chunk(row_sum, c), 1.0 / D, None,
                                      ALU.mult).then_inc(ln_mean, 1)
                    wait_step(dve, ln_mean, k)
                    dve.tensor_tensor(by_block(chunked(cent, c)), by_block(chunked(x_all, c)),
                                      spread(of_chunk(mean, c), D), ALU.subtract).then_inc(ln_cent, 1)
                return body

            def variance(n):
                def body(c, slot):
                    wait_step(dve, ln_sq, c + (n - 1) * CHUNKS)
                    dve.tensor_reduce(of_chunk(var, c), by_block(sq[:, slot, :]), AX_X, ALU.add).then_inc(ln_var, 1)
                return body

            def normalise(n, c, to, staged):
                k = c + (n - 1) * CHUNKS
                wait_step(dve, ln_std, k)
                dve.reciprocal(of_chunk(rstd, c), of_chunk(std, c)).then_inc(ln_rstd, 1)
                wait_step(dve, ln_rstd, k)
                dve.scalar_tensor_tensor(out=by_block(to), in0=by_block(chunked(cent, c)), scalar=0.0,
                                         in1=spread(of_chunk(rstd, c), D), op0=ALU.max,
                                         op1=ALU.mult).then_inc(staged, 1)

            def stage_h(c, slot):
                wait_step(dve, h_turned, c - 2)
                normalise(1, c, h_stage[:, slot, :], h_staged)

            dve.wait_ge(x_begun, 16)
            piped(dve, CHUNKS, 2, ((1, variance(1)), (0, centre(1)), (1, stage_h)),
                  lambda: dve.wait_ge(x_loaded, 16 * (CHUNKS // 2 - 1)))

            def keep(k, to):
                h = k % 2
                g0, n = h * HALF[0], HALF[h]
                for q in range(2):
                    dve.wait_ge(key_turned, 2 * k + q + 1)
                    dve.tensor_copy(to[:, g0:g0 + n, 4 * q:4 * q + 4].rearrange("p g t -> p t g"),
                                    pair[3][:, q, :].rearrange("p (t g) -> p t g", g=P)[:, :, 0:n]).then_inc(key_kept, 1)

            dve.wait_ge(consts_set, 5)
            dve.wait_ge(dst_loaded, 48)
            for h in range(2):
                n = HALF[h]
                dve.tensor_reduce(hi[0:n, h:h + 1], dst_i[0:n, h, :], AX_X, ALU.max).then_inc(range_made, 1)
                dve.tensor_reduce(lo[0:n, h:h + 1], dst_i[0:n, h, :], AX_X, ALU.min).then_inc(range_made, 1)
                dve.tensor_copy(base[0:n, h:h + 1], dst_i[0:n, h, 0:1]).then_inc(range_made, 1)
            dve.wait_ge(range_made, 6)
            for h in range(2):
                n = HALF[h]
                dve.scalar_tensor_tensor(out=above[0:n, h:h + 1], in0=hi[0:n, h:h + 1], scalar=1.0 - W,
                                         in1=base[0:n, h:h + 1], op0=ALU.add, op1=ALU.is_gt).then_inc(above_made, 1)
            dve.wait_ge(above_made, 2)
            for h in range(2):
                n = HALF[h]
                dve.scalar_tensor_tensor(out=bad[0:n, h:h + 1], in0=lo[0:n, h:h + 1], scalar=base[0:n, h:h + 1],
                                         in1=above[0:n, h:h + 1], op0=ALU.is_lt, op1=ALU.add).then_inc(bad_made, 1)
            n = HALF[1]

            def tiles(ap):
                return ap.rearrange("g (t e) -> g t e", t=T)

            dve.tensor_copy(t_base[:, :], tiles(dst_i[0:n, 1, :])[:, :, 0]).then_inc(t_base_made, 1)
            dve.wait_ge(t_base_made, 1)
            dve.tensor_tensor(tiles(d_key), tiles(dst_i[0:n, 1, :]),
                              t_base[:, :].rearrange("g (t o) -> g t o", o=1).to_broadcast([n, T, P]),
                              ALU.subtract).then_inc(t_rel_made, 1)
            dve.wait_ge(t_rel_made, 1)
            dve.tensor_reduce(t_hi[:, :], d_key, AX_X, ALU.max).then_inc(t_range_made, 1)
            dve.tensor_reduce(t_lo[:, :], d_key, AX_X, ALU.min).then_inc(t_range_made, 1)
            dve.wait_ge(t_range_made, 2)
            dve.tensor_scalar(t_above[:, :], t_hi[:, :], WT - 0.5, None, ALU.is_gt).then_inc(t_above_made, 1)
            dve.wait_ge(t_above_made, 1)
            dve.scalar_tensor_tensor(out=bad[0:n, 2:3], in0=t_lo[:, :], scalar=0.0, in1=t_above[:, :],
                                     op0=ALU.is_lt, op1=ALU.add).then_inc(bad_made, 1)
            dve.wait_ge(w2_turned, 1)
            dve.tensor_copy(w2bT[:, :], pair[3][0:D, 0, 0:D + 1]).then_inc(w2_kept, 1)
            dve.wait_ge(w2u_made, 1)
            dve.tensor_copy(w2u[:, :], pair[3][0:D + 1, 1, 0:D]).then_inc(w2u_kept, 1)
            dve.wait_ge(bad_summed, 1)
            dve.tensor_reduce(bad_all[:, :], pair[3][:, 0, 0:3], AX_X, ALU.add).then_inc(bad_counted, 1)
            dve.wait_ge(bad_counted, 1)
            dve.tensor_scalar(fast_f[:, :], bad_all[:, :], 0.5, None, ALU.is_lt).then_inc(fast_made, 1)
            dve.wait_ge(fast_made, 1)
            dve.tensor_copy(fast_i[:, :], fast_f[:, :]).then_inc(fast_made, 1)
            for h in range(2):
                dve.tensor_tensor(base[0:HALF[h], h:h + 1], base[0:HALF[h], h:h + 1], fast_f[0:HALF[h], :],
                                  ALU.mult).then_inc(range_made, 1)
            for k in range(2, 4):
                n = HALF[k - 2]
                dve.wait_ge(key_turned, 2 * k)
                dve.wait_ge(range_made, 7 + k - 2)
                made = dve.tensor_scalar(key_g[0:n, :], dst_i[0:n, k - 2, :], base[0:n, k - 2:k - 1], None, ALU.subtract)
                if k == 2:
                    made.then_inc(last_made, 1)
                    dve.wait_ge(last_made, 1)
                    dve.memset(key_g[0:1, 0:OVERLAP], FAR).then_inc(key_made, 1)
                else:
                    made.then_inc(key_made, 1)
            def rest_of_tables():
                for k in range(4, 6):
                    keep(k, wgt)
                n = HALF[1]
                dve.tensor_scalar(d_hi, src_i[0:n, 1, :], 7, None, ALU.arith_shift_right).then_inc(t_hi_made, 1)
                dve.wait_ge(t_hi_made, 1)
                dve.scalar_tensor_tensor(out=d_key, in0=d_hi, scalar=float(WT), in1=d_key, op0=ALU.mult,
                                         op1=ALU.add).then_inc(key_made, 1)
                dve.wait_ge(key_made, 5)
                dve.tensor_scalar(d_hi, src_i[0:n, 1, :], P - 1, None, ALU.bitwise_and).then_inc(t_lo_made, 1)
                dve.wait_ge(t_lo_made, 1)
                dve.wait_ge(key_turned, 8)
                dve.tensor_copy(key_g[0:n, :], d_hi).then_inc(key_made, 1)

                def keep_tiles(k, to):
                    for q in range(2):
                        dve.wait_ge(key_turned, 2 * k + q + 1)
                        dve.tensor_copy(to[:, 4 * q:4 * q + 4, :],
                                        pair[3][0:to.shape[0], q, :].rearrange("p (t g) -> p t g", g=P)[:, :, 0:n]
                                        ).then_inc(key_kept, 1)

                keep_tiles(6, by_turn(tile_key))
                keep_tiles(7, by_turn(tile_lo))
                keep_tiles(8, by_turn(tile_w[:, 0, :]))
                keep_tiles(9, by_turn(tile_row[:, :]))
                dve.wait_ge(key_kept, 18)
                for k in range(PARTS - 1):
                    if k:
                        dve.wait_ge(w_split, 3 * k)
                    dve.tensor_copy(tile_wb, tile_w[:, k, :]).then_inc(w_split, 1)
                    dve.wait_ge(w_split, 3 * k + 1)
                    dve.tensor_tensor(tile_w[:, k + 1, :], tile_w[:, k, :], tile_wb,
                                      ALU.subtract).then_inc(w_split, 1)
                    dve.wait_ge(w_split, 3 * k + 2)
                    dve.tensor_copy(tile_w[:, k, :], tile_wb).then_inc(w_split, 1)

            dve.wait_ge(base_made, 1)
            dve.wait_ge(fast_made, 2)
            dve.wait_ge(consts_set, 13)
            dve.wait_ge(key_kept, 8)
            fast = dve.value_load(fast_i[0:1, 0:1], min_val=0, max_val=1)

            iota_bc = iota[:, :].rearrange("p (o w) -> p o w", o=1).to_broadcast([P, T, W])

            def over_window(ap):
                return ap.rearrange("p (t o) -> p t o", o=1).to_broadcast([P, T, W])

            def at_group(table, g):
                return table[:, g, :] if isinstance(g, int) else table[:, ds(g, 1), :].rearrange("p o t -> p (o t)")

            def add_product(g, slot):
                gathered_wait(dve, g, slot, 0)
                wait_step(dve, q_made, g)
                wait_step(dve, hid_made, g - RING)
                dve.tensor_tensor(pre[:, slot, :, :], rows[:, slot, :, :],
                                  pair[slot][:, 1, :].rearrange("p (t f) -> p t f", f=D), ALU.add).then_inc(pre_made, 1)

            def accumulate(acc, m, start, n, done):
                to = acc[:, ds(start, W)]
                dve.tensor_tensor(to, to, pair[3][0:m, 0, 0:W], ALU.add).then_inc(done, 1)

            def fast1(g, slot):
                wait_step(dve, group_done, g - RING)
                dve.tensor_tensor(hot[:, slot, :, :], iota_bc, over_window(at_group(rel, g)),
                                  ALU.is_equal).then_inc(hot_made, 1)
                start = dve.value_load(base_row[0:1, ds(g, 1)], min_val=0, max_val=N)
                add_product(g, slot)
                wait_step(dve, group_done, g)
                wait_step(dve, acc_added, g - 1)
                accumulate(acc1, D + 1, start, g, acc_added)

            def group_hot(g, slot):
                wait_step(dve, group_done, g - RING + GROUPS)
                dve.tensor_tensor(hot[:, slot, :, :], iota_bc, over_window(at_group(rel, g)),
                                  ALU.is_equal).then_inc(hot_made, 1)
                wait_step(dve, hot_made, g + GROUPS)
                dve.tensor_tensor(hot[:, slot, :, :], hot[:, slot, :, :], over_window(at_group(wgt, g)),
                                  ALU.mult).then_inc(hot_weighed, 1)

            def add_group(g, bank):
                start = dve.value_load(base_row[0:1, ds(g, 1)], min_val=0, max_val=N)
                wait_step(dve, group_done, g + GROUPS)
                wait_step(dve, acc_added, g - 1 + GROUPS)
                to = acc2[:, ds(start, W)]
                dve.tensor_tensor(to, to, pair[3][0:D, bank, 0:W], ALU.add).then_inc(acc_added, 1)

            def tile_bases(i, n):
                return nc.values_load_multi_w_load_instructions(
                    tile_row[0:1, ds(i, n)],
                    engines=[mybir.EngineType.DVE], min_val=0, max_val=N,
                    skip_runtime_bounds_check_because="they are destination nodes, and acc2 is a window wider")[1]

            def add_tile(start, i, bank):
                to = acc2[:, ds(start, WT)]
                dve.tensor_tensor(to, to, pair[2][0:D, bank, i * WT:(i + 1) * WT], ALU.add).then_inc(tile_added, 1)

            def end_batch():
                dve.wait_ge(tile_added, BATCH)
                dve.sem_clear(tile_added)
                dve.sem_inc(batch_added, 1)

            def stage_columns(j, b):
                dve.tensor_copy(tile_now[:, b, :, :], tile_tab[:, :, ds(j * BATCH, BATCH)]
                                ).then_inc(columns_staged, 1)

            HOT_AT = (0, 8, 14)
            ADD_AT = (3, 11, 19)
            BEHIND = 4

            def dense_turn(j, b):
                first = isinstance(j, int) and j < 2
                added = 0
                starts = []
                group_last = False
                dve.wait_ge(columns_staged, j + 1)
                for i in range(BATCH):
                    if i in HOT_AT:
                        u = HOT_AT.index(i)
                        group_hot(j * RING + u, u)
                    if i % 4 == 0:
                        made = j * PAIRS + i // 2 - 3
                        if not isinstance(j, int) or made > 0:
                            dve.wait_ge(pair_made, made)
                    key, lo, w0 = (tile_now[:, b, k, i:i + 1] for k in range(3))
                    dve.tensor_scalar(hot_key[:, i % DRING, :], iota_key[:, :], key, None, ALU.is_equal)
                    dve.tensor_scalar(hot_w[0][:, i % DRING, :], iota_key[:, 0:P], lo, w0, ALU.is_equal, ALU.mult)
                    last = dve.tensor_scalar(hot_eq[:, i % DRING, :], iota_key[:, 0:P], lo, None, ALU.is_equal)
                    if i % 2 == 1:
                        last.then_inc(pair_hot, 1)
                    if not first and i >= BEHIND:
                        if i == BEHIND:
                            dve.wait_ge(applied, j - 1)
                        for _ in range(1 + (i >= BATCH - BEHIND)):
                            if not starts:
                                starts = list(tile_bases((j - 2) * BATCH + added, min(4, BATCH - added)))
                            if group_last:
                                dve.wait_ge(acc_added, j * RING + ADD_AT.index(group_at) + GROUPS)
                            elif added:
                                dve.wait_ge(tile_added, added)
                            add_tile(starts.pop(0), added, b)
                            added += 1
                            group_last = False
                    if i in ADD_AT:
                        u = ADD_AT.index(i)
                        if not (isinstance(j, int) and j + u == 0):
                            if added:
                                dve.wait_ge(tile_added, added)
                            add_group(j * RING + u - 1, (b + u + 1) % 2)
                            group_last, group_at = True, i
                    if i == 12 and not (isinstance(j, int) and j == BATCHES - 1):
                        stage_columns(j + 1, 1 - b)
                if not first:
                    end_batch()

            def add_batch(b):
                dve.wait_ge(applied, b + 1)
                for i in range(0, BATCH, 4):
                    for k, start in enumerate(tile_bases(b * BATCH + i, min(4, BATCH - i))):
                        if i + k:
                            dve.wait_ge(tile_added, i + k)
                        add_tile(start, i + k, b % 2)
                end_batch()

            def rest(g, slot):
                group_hot(g, slot)
                add_group(g, 0)

            def windows(acc, m, g, slot, done, weigh):
                n0 = (g + done) * WINDOWS
                dve.tensor_copy(key_now[:, slot, :], at_group(rel, g)).then_inc(key_moved, 1)
                moved0 = (g + done) * (WINDOWS + 1)
                with dve.Fori(0, WINDOWS) as k:
                    dve.wait_ge(key_moved, moved0 + k + 1)
                    dve.tensor_tensor(hot[:, slot, :, :], iota_bc, over_window(key_now[:, slot, :]),
                                      ALU.is_equal).then_inc(whot_made, 1)
                    dve.wait_ge(whot_made, n0 + k + 1)
                    if weigh:
                        dve.tensor_tensor(hot[:, slot, :, :], hot[:, slot, :, :], over_window(at_group(wgt, g)),
                                          ALU.mult).then_inc(whot_weighed, 1)
                    dve.tensor_scalar(key_now[:, slot, :], key_now[:, slot, :], -float(W), None,
                                      ALU.add).then_inc(key_moved, 1)
                    dve.wait_ge(wseg_made, n0 + k + 1)
                    accumulate(acc, m, k * W, None, wacc_added)
                    dve.wait_ge(wacc_added, n0 + k + 1)

            def slow1(g, slot):
                add_product(g, slot)
                windows(acc1, D + 1, g, slot, 0, False)
                dve.wait_ge(group_done, g + 1)

            def slow2(g, slot):
                windows(acc2, D, g, slot, GROUPS, True)
                dve.wait_ge(group_done, g + 1 + GROUPS)

            with dve.If(fast > 0):
                steps(dve, FULL, RING, fast1, rest_of_tables)
                fast1(FULL, 0)
                dve.wait_ge(acc_added, GROUPS)
            with dve.Else():
                steps(dve, FULL, RING, slow1, rest_of_tables)
                slow1(FULL, 0)
            dve.nop().then_inc(turn_made, 1)


            def sum_g(c, slot):
                wait_step(dve, g_made, c)
                wait_step(dve, up_made, c - 2)
                dve.tensor_tensor(t_stage[0:D, slot, :].rearrange("f (b n) -> f b n", n=NP),
                                  hT[0:D, ds(c * CN, CN)].rearrange("f (b n) -> f b n", n=NP),
                                  wide(slot)[:, :, 0:NP], ALU.add).then_inc(g_summed, 1)

            dve.wait_ge(part_kept, 1 + NB)

            def add_up(c, slot):
                wait_step(dve, up_made, c)
                dve.tensor_tensor(chunked(x_all, c), chunked(x_all, c), tall(slot), ALU.add).then_inc(x1_made, 1)
                wait_step(dve, x1_made, c)

            def stage_h2(c, slot):
                normalise(2, c, chunked(row_all, c), h2_staged)

            piped(dve, CHUNKS, 2, ((0, sum_g), (2, variance(2)), (1, add_up), (1, centre(2)), (2, stage_h2)), alone=4)
            dve.wait_ge(batch_added, 1)

            with dve.If(fast > 0):
                stage_columns(0, 0)
                dense_turns(dve, dense_turn)
                add_group(RING * BATCHES - 1, (RING * BATCHES - 1) % 2)
                dve.wait_ge(acc_added, RING * BATCHES + GROUPS)
                add_batch(BATCHES - 2)
                rest_of_half(dve, rest)
                dve.wait_ge(acc_added, HALF[0] + GROUPS)
                add_batch(BATCHES - 1)
            with dve.Else():
                steps(dve, FULL, RING, slow2)
                slow2(FULL, 0)
            dve.nop().then_inc(turn_made, 1)

            def chunk3(c, slot):
                wait_step(dve, a_turned, c)
                dve.tensor_tensor(chunked(x_all, c), chunked(x_all, c), tall(slot),
                                  ALU.add).then_inc(out_staged, 1)

            steps(dve, CHUNKS, 2, chunk3)


_INS = ['x', 'src', 'dst', 'edge_attr_64', 'edge_weight', 'L0_gnn_W1', 'L0_gnn_b1', 'L0_gnn_W2', 'L0_gnn_b2',
        'L0_gnn_U1', 'L0_gnn_c1', 'L0_gnn_U2', 'L0_gnn_c2']


def kernel(**inputs):
    import numpy as _np
    import concourse.bacc as _bacc
    from concourse import mybir as _mybir
    from concourse.bass_utils import run_bass_kernel_spmd as _run

    nc = _bacc.Bacc("TRN2", target_bir_lowering=False, num_devices=1)
    arrays, args = {}, []
    for name in _INS:
        a = _np.ascontiguousarray(inputs[name])
        arrays[f"in_{name}_dram"] = a
        args.append(nc.dram_tensor(f"in_{name}_dram", a.shape, _mybir.dt.from_np(a.dtype), kind="ExternalInput").ap())
    shape = _np.asarray(inputs['x']).shape
    args.append(nc.dram_tensor("out_0_dram", shape, _mybir.dt.float32, kind="ExternalOutput").ap())
    build(nc, *args)
    r = _run(nc, [arrays], core_ids=[0])
    return r.results[0]["out_0_dram"]
```
